# Optimizing a Trainium2 kernel written in Bass

```python
import numpy as np
import jax
import jax.numpy as jnp

def _softmax(x, axis=-1):
    return jax.nn.softmax(x, axis=axis)

def _gelu(x):
    return jax.nn.gelu(x, approximate=True)

def _silu(x):
    return jax.nn.silu(x)

def _sigmoid(x):
    return jax.nn.sigmoid(x)

def _layernorm(x, axis=-1, eps=1e-05):
    m = jnp.mean(x, axis=axis, keepdims=True)
    v = jnp.var(x, axis=axis, keepdims=True)
    return (x - m) / jnp.sqrt(v + eps)

def _scatter_add(tgt, idx, src, axis=0):
    return tgt.at[idx].add(src)

def _segment_sum(src, seg, n):
    return jax.ops.segment_sum(src, seg, n)
kernel_name = 'mk_gnn_preln_d1_gnn_r32_9343e1'

def setup_inputs(seed: int=0):
    np.random.seed(seed)
    _w = jnp.asarray

    def _rec_inputs():
        import jax
        import jax.numpy as jnp
        _gk = jax.random.key(seed)
        x = -0.000202 + 1 * jax.random.normal(jax.random.fold_in(_gk, 1), (3125, 128), jnp.float32)
        _s = jax.random.randint(jax.random.fold_in(_gk, 2), (25000,), 0, 3125, jnp.int32)
        _d = jax.random.randint(jax.random.fold_in(_gk, 3), (25000,), 0, 3125, jnp.int32)
        _loop = jnp.arange(3125, dtype=jnp.int32)
        src = jnp.concatenate([_s, _d, _loop])
        dst = jnp.concatenate([_d, _s, _loop])
        _o = jnp.argsort(dst, stable=True)
        src = src[_o]
        dst = dst[_o]
        return (x, src, dst)
    x, src, dst = _rec_inputs()

    def _L0_gnn_setup():
        import jax, jax.numpy as jnp
        import numpy as np
        N_NODES = 50000
        N_EDGES = 20000
        H = 128
        NEG_SLOPE = 0.2
        EPS = 1e-16

        def _gat_conv(x, src, dst, W, a_src, a_dst, b, n):
            h = x @ W
            al_s = h @ a_src
            al_d = h @ a_dst
            e = jax.nn.leaky_relu(al_s[src] + al_d[dst], NEG_SLOPE)
            m = jax.ops.segment_max(e, dst, num_segments=n)
            ex = jnp.exp(e - m[dst])
            denom = jax.ops.segment_sum(ex, dst, num_segments=n)
            alpha = ex / (denom[dst] + EPS)
            out = jax.ops.segment_sum(alpha[:, None] * h[src], dst, num_segments=n)
            return out + b
        key = jax.random.key(seed)
        ks = jax.random.split(key, 10)
        s = 1.0 / np.sqrt(H)
        x = jax.random.normal(ks[0], (N_NODES, H), dtype=jnp.float32)
        edge_index = jax.random.randint(ks[1], (2, N_EDGES), 0, N_NODES, dtype=jnp.int32)
        enc_W = jax.random.normal(ks[2], (3, H, H), dtype=jnp.float32) * s
        enc_b = jnp.zeros((3, H), dtype=jnp.float32)
        conv_W = jax.random.normal(ks[3], (9, H, H), dtype=jnp.float32) * s
        conv_att_src = jax.random.normal(ks[4], (9, H), dtype=jnp.float32) * s
        conv_att_dst = jax.random.normal(ks[5], (9, H), dtype=jnp.float32) * s
        conv_b = jnp.zeros((9, H), dtype=jnp.float32)
        dec_W = jax.random.normal(ks[6], (3, H, H), dtype=jnp.float32) * s
        dec_b = jnp.zeros((3, H), dtype=jnp.float32)
        return dict(x=x, edge_index=edge_index, enc_W=enc_W, enc_b=enc_b, conv_W=conv_W, conv_att_src=conv_att_src, conv_att_dst=conv_att_dst, conv_b=conv_b, dec_W=dec_W, dec_b=dec_b)
    _L0_gnn_all = _L0_gnn_setup()
    _L0_gnn_in = {k: v for k, v in _L0_gnn_all.items() if k in ('enc_W', 'enc_b', 'conv_W', 'conv_att_src', 'conv_att_dst', 'conv_b', 'dec_W', 'dec_b')}
    del _L0_gnn_all
    return {'x': x, 'src': src, 'dst': dst, 'L0_gnn_enc_W': _L0_gnn_in['enc_W'], 'L0_gnn_enc_b': _L0_gnn_in['enc_b'], 'L0_gnn_conv_W': _L0_gnn_in['conv_W'], 'L0_gnn_conv_att_src': _L0_gnn_in['conv_att_src'], 'L0_gnn_conv_att_dst': _L0_gnn_in['conv_att_dst'], 'L0_gnn_conv_b': _L0_gnn_in['conv_b'], 'L0_gnn_dec_W': _L0_gnn_in['dec_W'], 'L0_gnn_dec_b': _L0_gnn_in['dec_b']}

def reference(x, src, dst, L0_gnn_enc_W, L0_gnn_enc_b, L0_gnn_conv_W, L0_gnn_conv_att_src, L0_gnn_conv_att_dst, L0_gnn_conv_b, L0_gnn_dec_W, L0_gnn_dec_b):
    import jax
    import jax.numpy as jnp

    def _L0_gnn_ref(x, edge_index, enc_W, enc_b, conv_W, conv_att_src, conv_att_dst, conv_b, dec_W, dec_b):
        import jax, jax.numpy as jnp
        import numpy as np
        N_NODES = 50000
        N_EDGES = 20000
        H = 128
        NEG_SLOPE = 0.2
        EPS = 1e-16

        def _gat_conv(x, src, dst, W, a_src, a_dst, b, n):
            h = x @ W
            al_s = h @ a_src
            al_d = h @ a_dst
            e = jax.nn.leaky_relu(al_s[src] + al_d[dst], NEG_SLOPE)
            m = jax.ops.segment_max(e, dst, num_segments=n)
            ex = jnp.exp(e - m[dst])
            denom = jax.ops.segment_sum(ex, dst, num_segments=n)
            alpha = ex / (denom[dst] + EPS)
            out = jax.ops.segment_sum(alpha[:, None] * h[src], dst, num_segments=n)
            return out + b
        n = x.shape[0]
        loop = jnp.arange(n, dtype=edge_index.dtype)
        src = jnp.concatenate([edge_index[0], loop])
        dst = jnp.concatenate([edge_index[1], loop])
        h = jax.nn.relu(x @ enc_W[0] + enc_b[0])
        h = jax.nn.relu(h @ enc_W[1] + enc_b[1])
        h = h @ enc_W[2] + enc_b[2]
        for i in range(9):
            h = jax.nn.relu(_gat_conv(h, src, dst, conv_W[i], conv_att_src[i], conv_att_dst[i], conv_b[i], n))
        h = jax.nn.relu(h @ dec_W[0] + dec_b[0])
        h = jax.nn.relu(h @ dec_W[1] + dec_b[1])
        h = h @ dec_W[2] + dec_b[2]
        return jax.nn.sigmoid(h)
    edge_index = jnp.stack([src, dst])
    h = jnp.maximum(_layernorm(x, axis=-1), 0.0)
    x = x + _L0_gnn_ref(h, edge_index, L0_gnn_enc_W, L0_gnn_enc_b, L0_gnn_conv_W, L0_gnn_conv_att_src, L0_gnn_conv_att_dst, L0_gnn_conv_b, L0_gnn_dec_W, L0_gnn_dec_b)
    return x

_drawn_inputs = setup_inputs


def setup_inputs(seed=0):
    import zlib

    import numpy as np

    out = dict(_drawn_inputs(seed))
    spreads = {'L0_gnn_enc_b': (0.0, 0.8), 'L0_gnn_conv_b': (0.0, 0.8), 'L0_gnn_dec_b': (0.0, 0.289)}
    factors = {'L0_gnn_enc_W': 8.0,
     'L0_gnn_conv_W': 7.075,
     'L0_gnn_conv_att_src': 8.0,
     'L0_gnn_conv_att_dst': 8.0}
    for name, (base, spread) in spreads.items():
        noise = np.random.default_rng([zlib.crc32(name.encode()), seed]).standard_normal(out[name].shape)
        drawn = base * np.exp(spread * noise) if base else spread * noise
        out[name] = jnp.asarray(drawn.astype(out[name].dtype))
    for name, factor in factors.items():
        out[name] = (out[name] * factor).astype(out[name].dtype)
    return out
```

```python
import concourse.bass as bass
from concourse import mybir
from contextlib import ExitStack

F32 = mybir.dt.float32
I32 = mybir.dt.int32
U32 = mybir.dt.uint32
I16 = mybir.dt.int16
BF16 = mybir.dt.bfloat16
ALU = mybir.AluOpType
ACT = mybir.ActivationFunctionType
AX = mybir.AxisListType.X

NODES, FEAT, EDGES, LAYERS = 3125, 128, 53125, 9
SLOPE, LN_EPS, SOFTMAX_EPS = 0.2, 1e-5, 1e-16

LANES = 125
TILES = NODES // LANES
CHUNKS = 5
PER = TILES // CHUNKS
WIDE = PER * LANES

GRAIN = 25
ROWS = EDGES // GRAIN
ROWS_PER_LANE = ROWS // LANES
EDGES_PER_LANE = EDGES // LANES
BLOCK = 20
BLOCKS = -(-NODES // BLOCK)
LAST_BASE = NODES - BLOCK
LAST_NEW = NODES - BLOCK * (BLOCKS - 1)
HALF = 80
WINDOW = 512
FETCHED = WINDOW - BLOCK
PASSES = WINDOW // 128
CODES = BLOCK * TILES
SHIFT = 12
NOWHERE = (1 << SHIFT) - 1
RING = 4

TINY = 2.0 ** -64
HUGE = 2.0 ** 64


def gat_program(nc, x, src, dst, enc_W, enc_b, conv_W, att_src, att_dst, conv_b, dec_W, dec_b, out):
    packed_d = nc.dram_tensor("packed_d", [EDGES + FETCHED], I32, kind="Internal").ap()
    firsts_d = nc.dram_tensor("firsts_d", [ROWS], F32, kind="Internal").ap()
    windows_d = nc.dram_tensor("windows_d", [ROWS, FETCHED], I32, kind="Internal").ap()
    counts_d = nc.dram_tensor("counts_d", [LANES, TILES, BLOCKS * BLOCK], F32, kind="Internal").ap()
    overlapping = bass.AP(tensor=packed_d.tensor, offset=0, ap=[[GRAIN, ROWS], [1, FETCHED]])

    top = ExitStack()
    with top:
        def sb(name, shape, dt=F32, stack=top):
            return stack.enter_context(nc.sbuf_tensor(name, shape, dt))

        def sem(name):
            return top.enter_context(nc.semaphore(name))

        ident = sb("ident", [128, 128])
        att_cols = sb("att_cols", [128, LAYERS, 2])
        whole = sb("whole", [1, 1], I32)
        whole_ready = sem("whole_ready")
        psum = top.enter_context(nc.psum_tensor("psum", [128, 8, 512], F32))

        resident = ExitStack()
        with resident:
            counts = sb("counts", [LANES, TILES, NODES], I16, resident)
            build_counts(nc, src, dst, conv_W, att_src, att_dst, packed_d, firsts_d, windows_d,
                         overlapping, counts, ident, att_cols, whole, whole_ready, psum, sem)
            network(nc, x, enc_W, enc_b, conv_W, conv_b, dec_W, dec_b, out, counts, None, ident, att_cols,
                    whole, whole_ready, psum, sem)

        build_counts_of_any(nc, src, dst, counts_d, whole, whole_ready, psum, lambda name: sem("any_" + name))
        network(nc, x, enc_W, enc_b, conv_W, conv_b, dec_W, dec_b, out, None, counts_d, ident, att_cols,
                whole, whole_ready, psum, lambda name: sem("any_" + name))


def taken(engine, whole, whole_ready, when):
    engine.wait_ge(whole_ready, 1)
    return engine.If(engine.value_load(whole[0:1, 0:1], min_val=0, max_val=1) == when)


def build_counts(nc, src, dst, conv_W, att_src, att_dst, packed_d, firsts_d, windows_d,
                 overlapping, counts, ident, att_cols, whole, whole_ready, psum, sem):
    scope = ExitStack()
    with scope:
        def sb(name, shape, dt=F32):
            return scope.enter_context(nc.sbuf_tensor(name, shape, dt))

        edges = sb("edges", [LANES, 2, EDGES_PER_LANE], I32)
        packed = sb("packed", [LANES, EDGES_PER_LANE], I32)
        firsts = sb("firsts", [LANES, ROWS_PER_LANE])
        beyond = sb("beyond", [1, FETCHED], I32)
        all_firsts = sb("all_firsts", [HALF, ROWS])
        below = sb("below", [HALF, ROWS], BF16)
        base_i = sb("base_i", [HALF, 2], I32)
        base = sb("base", [HALF, 2])
        rows_below = sb("rows_below", [HALF, 2])
        own_code = sb("own_code", [HALF, 2])
        held = sb("held", [HALF, 2])
        ones = sb("window_ones", [HALF, 1])
        first_row = sb("first_row", [HALF, 2], U32)
        window = sb("window", [HALF, 2, WINDOW], I32)
        src_f = sb("src_f", [HALF, 2 * WINDOW])
        wrong = code_f = src_f
        tile_i = sb("tile_i", [HALF, 2 * WINDOW], I32)
        tile_f = sb("tile_f", [HALF, 2 * WINDOW])
        lane_f = sb("lane_f", [HALF, 2 * WINDOW])
        lane_t = sb("lane_t", [128, PASSES, 2 * HALF])
        code_t = sb("code_t", [128, PASSES, 2 * HALF])
        iota_i = sb("iota_i", [128, CODES], I16)
        lane_hot = sb("lane_hot", [128, PASSES, LANES], BF16)
        code_hot = sb("code_hot", [128, PASSES, CODES], BF16)
        weights = sb("weights", [128, FEAT])
        att = sb("att", [128, 2, FEAT])
        product = sb("product", [128, FEAT])
        att_pair = sb("att_pair", [128, 2])

        edges_in = sem("edges_in")
        packed_out = sem("packed_out")
        windows_out = sem("windows_out")
        firsts_in = sem("firsts_in")
        weights_in = sem("weights_in")
        window_in = [sem("window_in0"), sem("window_in1")]
        pool_setup = sem("pool_setup")
        step = sem("dve_step")
        held_ready = sem("held_ready")
        held_summed = sem("held_summed")
        att_step = sem("att_step")
        packed_ready = sem("packed_ready")
        firsts_ready = sem("firsts_ready")
        first_row_ready = sem("first_row_ready")
        split_ready = sem("split_ready")
        turned = sem("turned")
        turned_copied = sem("turned_copied")
        hot_ready = sem("hot_ready")
        hot_used = sem("hot_used")
        block_stored = sem("block_stored")
        block = scope.enter_context(nc.Block())

        @block.sync
        def _(sp):
            sp.dma_start(edges[:, 1, :], dst.rearrange("(p j) -> p j", p=LANES)).then_inc(edges_in, 16)
            sp.dma_start(edges[:, 0, :], src.rearrange("(p j) -> p j", p=LANES)).then_inc(edges_in, 16)
            sp.wait_ge(firsts_ready, 1)
            sp.dma_start(firsts_d.rearrange("(p j) -> p j", p=LANES), firsts[:, :]).then_inc(firsts_in, 16)
            sp.wait_ge(packed_ready, 1)
            sp.wait_ge(pool_setup, 2)
            sp.dma_start(packed_d[0:EDGES].rearrange("(p j) -> p j", p=LANES), packed[:, :]).then_inc(packed_out, 16)
            sp.dma_start(packed_d[EDGES:EDGES + FETCHED].rearrange("(a j) -> a j", a=1), beyond[:, :]).then_inc(packed_out, 16)
            sp.wait_ge(firsts_in, 16)
            sp.dma_start(all_firsts[:, :], firsts_d.rearrange("(a j) -> a j", a=1).broadcast_to([HALF, ROWS])).then_inc(firsts_in, 16)
            sp.wait_ge(packed_out, 32)
            sp.dma_start(windows_d[:, :], overlapping).then_inc(windows_out, 16)
            with sp.Fori(0, LAYERS) as l:
                sp.wait_ge(att_step, 3 * l + 1)
                sp.dma_start(weights[:, :], conv_W[bass.ds(l, 1), :, :].rearrange("l k n -> (l k) n")).then_inc(weights_in, 16)
                sp.dma_start(att[:, 0, :], att_src[bass.ds(l, 1), :].broadcast_to([128, FEAT])).then_inc(weights_in, 16)
                sp.dma_start(att[:, 1, :], att_dst[bass.ds(l, 1), :].broadcast_to([128, FEAT])).then_inc(weights_in, 16)
            sp.wait_ge(weights_in, 48 * LAYERS)

        @block.gpsimd
        def _(pool):
            nc.gpsimd.iota(base_i[:, :], [[BLOCK * HALF, 2]], base=0, channel_multiplier=BLOCK).then_inc(pool_setup, 1)
            nc.gpsimd.memset(beyond[:, :], NOWHERE << SHIFT).then_inc(pool_setup, 1)
            nc.gpsimd.iota(iota_i[:, :], [[1, CODES]], base=0, channel_multiplier=0,
                           allow_small_or_imprecise_dtypes=True).then_inc(pool_setup, 1)
            nc.gpsimd.memset(ident[:, :], 0.0).then_inc(pool_setup, 1)
            pool.wait_ge(pool_setup, 4)
            nc.gpsimd.affine_select(out=ident[:, :], in_=ident[:, :], compare_op=ALU.not_equal, fill=1.0,
                                    base=0, pattern=[[-1, 128]], channel_multiplier=1).then_inc(pool_setup, 1)
            both = (1 << SHIFT) + 1
            for k in range(2):
                nc.gpsimd.iota(window[:, k, FETCHED:WINDOW], [[both, BLOCK]], base=BLOCK * HALF * k * both,
                               channel_multiplier=BLOCK * both).then_inc(pool_setup, 1)
            pool.wait_ge(first_row_ready, 1)
            pool.wait_ge(windows_out, 16)
            for k in range(2):
                nc.gpsimd.indirect_dma_start(
                    out=window[:, k, 0:FETCHED], out_offset=None, in_=windows_d[:, :],
                    in_offset=bass.IndirectOffsetOnAxis(ap=first_row[:, k:k + 1], axis=0)).then_inc(window_in[k], 16)
            for k in range(2):
                pool.wait_ge(window_in[k], 16)

        @block.vector
        def _(dve):
            done = [0]

            def link(ins):
                done[0] += 1
                ins.then_inc(step, 1)
                dve.wait_ge(step, done[0])

            dve.wait_ge(edges_in, 32)
            nc.vector.tensor_copy(firsts[:, :], edges[:, 1, :].rearrange("p (r g) -> p r g", g=GRAIN)[:, :, 0]).then_inc(firsts_ready, 1)
            nc.vector.scalar_tensor_tensor(out=packed[:, :], in0=edges[:, 1, :], scalar=float(1 << SHIFT), in1=edges[:, 0, :],
                                           op0=ALU.mult, op1=ALU.add).then_inc(packed_ready, 1)
            dve.wait_ge(pool_setup, 1)
            link(nc.vector.tensor_copy(base[:, :], base_i[:, :]))
            link(nc.vector.tensor_scalar(own_code[:, :], base[:, :], float(LAST_BASE), 0.0, ALU.subtract, ALU.max))
            link(nc.vector.tensor_scalar(own_code[:, :], own_code[:, :], float(TILES), None, ALU.mult))
            link(nc.vector.tensor_scalar(base[:, :], base[:, :], float(LAST_BASE), None, ALU.min))
            dve.wait_ge(firsts_in, 32)
            for k in range(2):
                link(nc.vector.tensor_scalar(below[:, :], all_firsts[:, :], base[:, k:k + 1], None, ALU.is_lt, ALU.add,
                                             accum_out=rows_below[:, k:k + 1]))
            nc.vector.tensor_scalar(first_row[:, :], rows_below[:, :], -1.0, 0.0, ALU.add, ALU.max).then_inc(first_row_ready, 1)

            dve.wait_ge(step, done[0])
            nc.vector.memset(product[:, :], 0.0).then_inc(att_step, 1)
            dve.wait_ge(att_step, 1)
            with dve.Fori(0, LAYERS) as l:
                dve.wait_ge(weights_in, 48 * l + 48)
                for k in range(2):
                    nc.vector.tensor_tensor_reduce(out=product[:, :], in0=weights[:, :], in1=att[:, k, :], scale=1.0, scalar=0.0,
                                                   op0=ALU.mult, op1=ALU.add,
                                                   accum_out=att_pair[:, k:k + 1]).then_inc(att_step, 1)
                    dve.wait_ge(att_step, 3 * l + 2 + k)
                nc.vector.tensor_copy(att_cols[:, bass.ds(l, 1), :].rearrange("p l a -> p (l a)"), att_pair[:, :]).then_inc(att_step, 1)
                dve.wait_ge(att_step, 3 * l + 4)

            for k in range(2):
                dve.wait_ge(window_in[k], 16)
            dve.wait_ge(pool_setup, 7)
            flat = window[:, :, :].rearrange("p k w -> p (k w)")
            link(nc.vector.tensor_scalar(tile_i[:, :], flat, NOWHERE, None, ALU.bitwise_and))
            link(nc.vector.tensor_copy(src_f[:, :], tile_i[:, :]))
            link(nc.vector.tensor_scalar(tile_i[:, :], src_f[:, :], 0.5, 1.0 / LANES, ALU.add, ALU.mult))
            link(nc.vector.tensor_copy(tile_f[:, :], tile_i[:, :]))
            link(nc.vector.scalar_tensor_tensor(out=lane_f[:, :], in0=tile_f[:, :], scalar=-float(LANES), in1=src_f[:, :], op0=ALU.mult, op1=ALU.add))
            link(nc.vector.tensor_scalar(wrong[:, :], lane_f[:, :], 0.0, None, ALU.is_lt))
            link(nc.vector.tensor_tensor(tile_f[:, :], tile_f[:, :], wrong[:, :], ALU.subtract))
            nc.vector.scalar_tensor_tensor(out=lane_f[:, :], in0=wrong[:, :], scalar=float(LANES), in1=lane_f[:, :], op0=ALU.mult, op1=ALU.add).then_inc(split_ready, 1)
            dve.wait_ge(split_ready, 1)
            link(nc.vector.tensor_scalar(tile_i[:, :], flat, SHIFT, None, ALU.logical_shift_right))
            for k in range(2):
                half = slice(WINDOW * k, WINDOW * (k + 1))
                link(nc.vector.tensor_scalar(code_f[:, half], tile_i[:, half], base[:, k:k + 1], float(TILES), ALU.subtract, ALU.mult))
            nc.vector.tensor_tensor(code_f[:, :], code_f[:, :], tile_f[:, :], ALU.add).then_inc(split_ready, 1)

            dve.wait_ge(split_ready, 2)
            link(nc.vector.memset(ones[:, :], 1.0))
            for k in range(2):
                half = slice(WINDOW * k, WINDOW * (k + 1))
                link(nc.vector.tensor_scalar(tile_f[:, half], code_f[:, half], own_code[:, k:k + 1], None, ALU.is_ge))
                link(nc.vector.scalar_tensor_tensor(out=tile_f[:, half], in0=code_f[:, half], scalar=float(CODES), in1=tile_f[:, half],
                                                    op0=ALU.is_lt, op1=ALU.mult))
            nc.vector.tensor_reduce(out=held[:, :], in_=tile_f[:, :].rearrange("p (k w) -> p k w", k=2), axis=AX,
                                    op=ALU.add).then_inc(held_ready, 1)
            dve.wait_ge(held_summed, 1)
            link(nc.vector.tensor_reduce(out=held[0:1, 0:1], in_=psum[0:1, 6, 0:2], axis=AX, op=ALU.add))
            nc.vector.tensor_scalar(whole[:, :], held[0:1, 0:1], float(EDGES + NODES), None, ALU.is_equal).then_inc(whole_ready, 1)

            dve.wait_ge(turned_copied, 2)

            def one_hots(b, first=False):
                for j in range(PASSES):
                    if not first:
                        dve.wait_ge(hot_used, PASSES * b - PASSES + j + 1)
                    at = slice(b, b + 1) if isinstance(b, int) else bass.ds(b, 1)
                    nc.vector.tensor_scalar(lane_hot[:, j, :], iota_i[:, 0:LANES], lane_t[:, j, at], None, ALU.is_equal).then_inc(hot_ready, 1)
                    nc.vector.tensor_scalar(code_hot[:, j, :], iota_i[:, :], code_t[:, j, at], None, ALU.is_equal).then_inc(hot_ready, 1)

            one_hots(0, first=True)
            with dve.Fori(1, BLOCKS) as b:
                one_hots(b)

        @block.tensor
        def _(pe):
            pe.wait_ge(pool_setup, 5)
            for n, part in enumerate((lane_f, code_f)):
                pe.wait_ge(split_ready, n + 1)
                for j in range(PASSES):
                    for k in range(2):
                        at = WINDOW * k + 128 * j
                        last = nc.tensor.transpose(psum[:, 2 * n + j // 2, 256 * (j % 2) + HALF * k:256 * (j % 2) + HALF * (k + 1)],
                                                   part[:, at:at + 128], ident[0:HALF, 0:HALF])
                last.then_inc(turned, 1)
            pe.wait_ge(held_ready, 1)
            nc.tensor.matmul(psum[0:1, 6, 0:2], ones[:, :], held[:, :], start=True, stop=True).then_inc(held_summed, 1)

            def count(b, bank):
                for j in range(PASSES):
                    pe.wait_ge(hot_ready, 2 * PASSES * b + 2 * j + 2)
                    last = nc.tensor.matmul(psum[0:LANES, bank, 0:CODES], lane_hot[:, j, :], code_hot[:, j, :],
                                            start=j == 0, stop=j == PASSES - 1)
                    last.then_inc(hot_used, 1)

            count(0, 4)
            count(1, 5)
            with pe.Fori(1, (BLOCKS - 1) // 2) as pair:
                for odd in range(2):
                    pe.wait_ge(block_stored, 2 * pair - 1 + odd)
                    count(2 * pair + odd, 4 + odd)
            pe.wait_ge(block_stored, BLOCKS - 2)
            count(BLOCKS - 1, 4)

        @block.scalar
        def _(act):
            for n, part in enumerate((lane_t, code_t)):
                act.wait_ge(turned, n + 1)
                nc.scalar.activation(part[:, :, :].rearrange("p (a b) c -> p a b c", a=2),
                                     psum[:, 2 * n:2 * n + 2, :].rearrange("p a (b c) -> p a b c", b=2)[:, :, :, 0:2 * HALF],
                                     ACT.Copy).then_inc(turned_copied, 1)

            def store(bank, at, first_dst, dsts, number):
                act.wait_ge(hot_used, number * PASSES)
                nc.scalar.activation(counts[:, :, at].rearrange("p t i -> p i t"),
                                     psum[0:LANES, bank, first_dst * TILES:(first_dst + dsts) * TILES].rearrange("p (i t) -> p i t", t=TILES),
                                     ACT.Copy, scale=2.0, bias=-1.0).then_inc(block_stored, 1)

            with act.Fori(0, (BLOCKS - 1) // 2) as pair:
                for odd in range(2):
                    store(4 + odd, bass.ds(2 * BLOCK * pair + BLOCK * odd, BLOCK), 0, BLOCK, 2 * pair + odd + 1)
            store(4, slice(NODES - LAST_NEW, NODES), BLOCK - LAST_NEW, LAST_NEW, BLOCKS)


def build_counts_of_any(nc, src, dst, counts_d, whole, whole_ready, psum, sem):
    scope = ExitStack()
    with scope:
        def sb(name, shape, dt=F32):
            return scope.enter_context(nc.sbuf_tensor("any_" + name, shape, dt))

        COLUMNS = EDGES_PER_LANE + TILES
        src_i = sb("src_i", [LANES, COLUMNS], I32)
        dst_i = sb("dst_i", [LANES, COLUMNS], I32)
        tile_i = sb("tile_i", [LANES, COLUMNS], I32)
        src_f = sb("src_f", [LANES, COLUMNS])
        wrong = src_f
        tile_f = sb("tile_f", [LANES, COLUMNS])
        lane_f = sb("lane_f", [LANES, COLUMNS])
        code_f = sb("code_f", [LANES, COLUMNS])
        iota_i = sb("iota_i", [LANES, CODES], I16)
        lane_hot = sb("lane_hot", [LANES, LANES], BF16)
        code_hot = sb("code_hot", [LANES, CODES], BF16)
        block_counts = sb("block_counts", [LANES, TILES, BLOCK])

        edges_in = sem("edges_in")
        loops_set = sem("loops_set")
        step = sem("dve_step")
        hot_ready = sem("hot_ready")
        hot_used = sem("hot_used")
        block_copied = sem("block_copied")
        block_stored = sem("block_stored")
        block = scope.enter_context(nc.Block())

        @block.sync
        def _(sp):
            with taken(sp, whole, whole_ready, 0):
                sp.dma_start(dst_i[:, 0:EDGES_PER_LANE], dst.rearrange("(p j) -> p j", p=LANES)).then_inc(edges_in, 16)
                sp.dma_start(src_i[:, 0:EDGES_PER_LANE], src.rearrange("(p j) -> p j", p=LANES)).then_inc(edges_in, 16)
                with sp.Fori(0, BLOCKS) as b:
                    sp.wait_ge(block_copied, b + 1)
                    sp.dma_start(counts_d[:, :, bass.ds(BLOCK * b, BLOCK)], block_counts[:, :, :]).then_inc(block_stored, 16)
                sp.wait_ge(block_stored, 16 * BLOCKS)

        @block.gpsimd
        def _(pool):
            with taken(pool, whole, whole_ready, 0):
                for ends in (src_i, dst_i):
                    nc.gpsimd.iota(ends[:, EDGES_PER_LANE:COLUMNS], [[LANES, TILES]], base=0, channel_multiplier=1).then_inc(loops_set, 1)
                nc.gpsimd.iota(iota_i[:, :], [[1, CODES]], base=0, channel_multiplier=0,
                               allow_small_or_imprecise_dtypes=True).then_inc(loops_set, 1)

        @block.vector
        def _(dve):
            with taken(dve, whole, whole_ready, 0):
                done = [0]

                def link(ins):
                    done[0] += 1
                    ins.then_inc(step, 1)
                    dve.wait_ge(step, done[0])

                dve.wait_ge(edges_in, 32)
                dve.wait_ge(loops_set, 3)
                link(nc.vector.tensor_copy(src_f[:, :], src_i[:, :]))
                link(nc.vector.tensor_copy(code_f[:, :], dst_i[:, :]))
                link(nc.vector.tensor_scalar(tile_i[:, :], src_f[:, :], 0.5, 1.0 / LANES, ALU.add, ALU.mult))
                link(nc.vector.tensor_copy(tile_f[:, :], tile_i[:, :]))
                link(nc.vector.scalar_tensor_tensor(out=lane_f[:, :], in0=tile_f[:, :], scalar=-float(LANES), in1=src_f[:, :], op0=ALU.mult, op1=ALU.add))
                link(nc.vector.tensor_scalar(wrong[:, :], lane_f[:, :], 0.0, None, ALU.is_lt))
                link(nc.vector.tensor_tensor(tile_f[:, :], tile_f[:, :], wrong[:, :], ALU.subtract))
                link(nc.vector.scalar_tensor_tensor(out=lane_f[:, :], in0=wrong[:, :], scalar=float(LANES), in1=lane_f[:, :], op0=ALU.mult, op1=ALU.add))
                link(nc.vector.scalar_tensor_tensor(out=code_f[:, :], in0=code_f[:, :], scalar=float(TILES), in1=tile_f[:, :], op0=ALU.mult, op1=ALU.add))

                def one_hots(j):
                    at = slice(j, j + 1) if isinstance(j, int) else bass.ds(j, 1)
                    nc.vector.tensor_scalar(lane_hot[:, :], iota_i[:, 0:LANES], lane_f[:, at], None, ALU.is_equal).then_inc(hot_ready, 1)
                    nc.vector.tensor_scalar(code_hot[:, :], iota_i[:, :], code_f[:, at], None, ALU.is_equal).then_inc(hot_ready, 1)

                def one_block(b):
                    if not isinstance(b, int):
                        dve.wait_ge(hot_used, COLUMNS * b)
                        nc.vector.tensor_scalar(code_f[:, :], code_f[:, :], float(CODES), None, ALU.subtract).then_inc(step, 1)
                        dve.wait_ge(step, b + done[0])
                    one_hots(0)
                    with dve.Fori(1, COLUMNS) as j:
                        dve.wait_ge(hot_used, COLUMNS * b + j)
                        one_hots(j)

                one_block(0)
                with dve.Fori(1, BLOCKS) as b:
                    one_block(b)

        @block.tensor
        def _(pe):
            def add_column(b, j):
                pe.wait_ge(hot_ready, 2 * (COLUMNS * b + j) + 2)
                fixed = isinstance(j, int)
                nc.tensor.matmul(psum[0:LANES, 4, 0:CODES], lane_hot[:, :], code_hot[:, :], start=fixed and j == 0,
                                 stop=fixed and j > 0, skip_group_check=True).then_inc(hot_used, 1)

            def one_block(b):
                if not isinstance(b, int):
                    pe.wait_ge(block_copied, b)
                add_column(b, 0)
                with pe.Fori(1, COLUMNS - 1) as j:
                    add_column(b, j)
                add_column(b, COLUMNS - 1)

            with taken(pe, whole, whole_ready, 0):
                one_block(0)
                with pe.Fori(1, BLOCKS) as b:
                    one_block(b)

        @block.scalar
        def _(act):
            def one_block(b):
                act.wait_ge(hot_used, COLUMNS * b + COLUMNS)
                if not isinstance(b, int):
                    act.wait_ge(block_stored, 16 * b)
                nc.scalar.activation(block_counts[:, :, :].rearrange("p t i -> p i t"),
                                     psum[0:LANES, 4, 0:CODES].rearrange("p (i t) -> p i t", t=TILES),
                                     ACT.Copy, scale=2.0, bias=-1.0).then_inc(block_copied, 1)

            with taken(act, whole, whole_ready, 0):
                one_block(0)
                with act.Fori(1, BLOCKS) as b:
                    one_block(b)


def network(nc, x, enc_W, enc_b, conv_W, conv_b, dec_W, dec_b, out, counts, counts_d, ident, att_cols,
            whole, whole_ready, psum, sem):
    scope = ExitStack()
    with scope:
        streamed = counts is None
        when = 0 if streamed else 1

        def sb(name, shape, dt=F32):
            return scope.enter_context(nc.sbuf_tensor("any_" + name if streamed else name, shape, dt))

        hidden = sb("hidden", [128, 2, TILES, FEAT + 1])
        al = sb("al", [LANES, 2, TILES, 2])
        al_tiny = sb("al_tiny", [LANES, 2, TILES])
        al_minus = sb("al_minus", [LANES, 2, TILES])
        al_fifth = sb("al_fifth", [LANES, 2, TILES])
        ring = sb("ring", [128, RING, WIDE])
        rows = sb("rows", [LANES, 2, 2 * WIDE])
        largest = sb("largest", [LANES, WIDE])
        node_major = sb("node_major", [LANES, PER, FEAT])
        feat_major = sb("feat_major", [128, WIDE])
        weights = sb("layer_weights", [128, FEAT + 2])
        peak = sb("peak", [LANES, PER])
        z_col = sb("z_col", [LANES, PER])
        row_cols = sb("row_cols", [LANES, 2, PER])
        denom = sb("denom", [LANES, PER])
        conv_bias = sb("conv_bias", [128, LAYERS])
        enc_bias = sb("enc_bias", [128, 3])
        dec_bias = sb("dec_bias", [128, 3])
        stats = sb("stats", [LANES, PER, 6])
        moments = sb("moments", [LANES, PER, 2])
        spread = sb("spread", [LANES, 3, PER])

        enc_w = ring[:, 0, 0:3 * FEAT].rearrange("p (k n) -> p k n", k=3)
        x_all = hidden[0:LANES, 1, :, 0:FEAT]
        spare = hidden[:, LAYERS % 2, :, :].rearrange("p t f -> p (t f)")
        dec_w = spare[:, 0:3 * FEAT].rearrange("p (k n) -> p k n", k=3)
        x_chunk = spare[0:LANES, 384:384 + PER * FEAT]
        result = spare[0:LANES, 1024:1024 + PER * FEAT]
        dec_row = spare[0:1, 1664:1664 + FEAT]
        one_row = spare[0:1, 1800:1800 + LANES]

        if streamed:
            max_tile = sb("max_tile", [LANES, WIDE])
            weigh_tile = sb("weigh_tile", [LANES, WIDE])
            max_tile_in = sem("max_tile_in")
            weigh_tile_in = sem("weigh_tile_in")

        consts_in = sem("consts_in")
        x_in = [sem(f"x_in{c}") for c in range(CHUNKS)]
        weights_in = sem("layer_weights_in")
        dec_in = sem("dec_in")
        x_again = sem("x_again")
        stored = sem("stored")
        ones_set = sem("ones_set")
        ln_step = sem("ln_step")
        variance_ready = sem("variance_ready")
        root_ready = sem("root_ready")
        nodes_ready = sem("nodes_ready")
        nodes_turned = sem("nodes_turned")
        feats_ready = sem("feats_ready")
        dense_ready = sem("dense_ready")
        dense_copied = sem("dense_copied")
        hidden_mm = sem("hidden_mm")
        hidden_ready = sem("hidden_ready")
        al_ready = sem("al_ready")
        al_scaled = sem("al_scaled")
        maxed = sem("maxed")
        largest_turned = sem("largest_turned")
        col_step = sem("col_step")
        col_done = sem("col_done")
        cols_ready = sem("cols_ready")
        rows_spread = sem("rows_spread")
        rows_ready = sem("rows_ready")
        distance_ready = sem("distance_ready")
        exponent_ready = sem("exponent_ready")
        clamped = sem("clamped")
        exp_ready = sem("exp_ready")
        weight_ready = sem("weight_ready")
        tile_used = sem("tile_used")
        denom_step = sem("denom_step")
        denom_ready = sem("denom_ready")
        sigmoid_ready = sem("sigmoid_ready")
        result_ready = sem("result_ready")
        block = scope.enter_context(nc.Block())

        SUMS, FINISH, START = 0, 2, 4
        PER_BANK = 512 // LANES

        def piece(bank, i, n=LANES):
            return psum[0:n, bank + i // PER_BANK, LANES * (i % PER_BANK):LANES * (i % PER_BANK) + LANES]

        def sums(i, a=0, b=FEAT + 1):
            at = (FEAT + 1) * (i % 3)
            return psum[0:LANES, SUMS + i // 3, at + a:at + b]

        def fresh(i, a, b):
            n = 3 - i
            return psum[0:LANES, FINISH + i, 0:n * (FEAT + 2)].rearrange("p (t f) -> p t f", f=FEAT + 2)[:, :, a:b]

        def when_max_runs(own):
            return [list(range(own * s // 20, own * (s + 1) // 20)) if s < 20 else [] for s in range(TILES)]

        def max_plan(more, last_layer):
            return when_max_runs(TILES if more else 20 if not last_layer else 0)

        AFTER = 20
        node_rows = lambda c: slice(c * WIDE, (c + 1) * WIDE)

        @block.sync
        def _(sp):
            with taken(sp, whole, whole_ready, when):
                for c in range(CHUNKS):
                    sp.dma_start(x_all[:, PER * c:PER * (c + 1), :],
                                 x[node_rows(c), :].rearrange("(t p) f -> p t f", p=LANES)).then_inc(x_in[c], 16)
                sp.dma_start(enc_w, enc_W.rearrange("k i n -> i k n")).then_inc(consts_in, 16)
                sp.dma_start(enc_bias[:, :], enc_b.rearrange("k f -> f k"), allow_slow_non_contiguous=True).then_inc(consts_in, 16)
                sp.dma_start(dec_bias[:, :], dec_b.rearrange("k f -> f k"), allow_slow_non_contiguous=True).then_inc(consts_in, 16)
                sp.dma_start(conv_bias[:, :], conv_b.rearrange("k f -> f k"), allow_slow_non_contiguous=True).then_inc(consts_in, 16)

                def load_tile(tile, loaded, used, l, c, t):
                    n = TILES * (CHUNKS * l + c) + t
                    if not (isinstance(n, int) and n == 0):
                        sp.wait_ge(used, n)
                    sp.dma_start(tile[:, :], counts_d[:, t, chunk_columns(c)]).then_inc(loaded, 16)

                def load_max(l, c, t):
                    load_tile(max_tile, max_tile_in, maxed, l, c, t)

                def stream_step(l, c):
                    more, last_layer = c < CHUNKS - 1, isinstance(l, int) and l == LAYERS - 1
                    for t, maxima in enumerate(max_plan(more, last_layer)):
                        load_tile(weigh_tile, weigh_tile_in, weight_ready, l, c, t)
                        for a in maxima:
                            load_max(*((l, c + 1) if more else (l + 1, 0)), a)
                    if not more and not last_layer:
                        for a in range(20, TILES):
                            load_max(l + 1, 0, a)

                def load_weights(k):
                    at = slice(k, k + 1) if isinstance(k, int) else bass.ds(k, 1)
                    sp.dma_start(weights[:, 0:FEAT], conv_W[at, :, :].rearrange("l k n -> (l k) n")).then_inc(weights_in, 16)
                    sp.dma_start(weights[:, FEAT:FEAT + 2], att_cols[:, at, :].rearrange("p l a -> p (l a)")).then_inc(weights_in, 16)

                load_weights(0)
                if streamed:
                    for t in range(TILES):
                        load_max(0, 0, t)

                def layer(l):
                    sp.wait_ge(hidden_mm, CHUNKS * l + CHUNKS)
                    load_weights(l + 1)
                    if streamed:
                        for c in range(CHUNKS):
                            stream_step(l, c)

                layer(0)
                with sp.Fori(1, LAYERS - 1) as l:
                    layer(l)
                sp.wait_ge(tile_used, TILES * CHUNKS * (LAYERS - 1) + TILES)
                sp.wait_ge(hidden_ready, CHUNKS * LAYERS)
                sp.dma_start(dec_w, dec_W.rearrange("k i n -> i k n")).then_inc(dec_in, 16)
                sp.dma_start(dec_row, dec_b[2:3, :]).then_inc(dec_in, 16)
                for c in range(CHUNKS):
                    if streamed:
                        stream_step(LAYERS - 1, c)
                    if c:
                        sp.wait_ge(result_ready, c)
                        sp.dma_start(out[node_rows(c - 1), :].rearrange("(t p) f -> p t f", p=LANES),
                                     result.rearrange("p (t f) -> p t f", f=FEAT)).then_inc(stored, 16)
                    sp.dma_start(x_chunk.rearrange("p (t f) -> p t f", f=FEAT),
                                 x[node_rows(c), :].rearrange("(t p) f -> p t f", p=LANES)).then_inc(x_again, 16)
                sp.wait_ge(result_ready, CHUNKS)
                sp.dma_start(out[node_rows(CHUNKS - 1), :].rearrange("(t p) f -> p t f", p=LANES),
                             result.rearrange("p (t f) -> p t f", f=FEAT)).then_inc(stored, 16)
                sp.wait_ge(stored, 16 * CHUNKS)

        @block.gpsimd
        def _(pool):
            with taken(pool, whole, whole_ready, when):
                nc.gpsimd.memset(hidden[:, 0, :, FEAT:FEAT + 1], 1.0).then_inc(ones_set, 1)
                nc.gpsimd.memset(hidden[:, 1, :, FEAT:FEAT + 1], 1.0).then_inc(ones_set, 1)
                pool.wait_ge(tile_used, TILES * CHUNKS * (LAYERS - 1) + TILES)
                nc.gpsimd.memset(one_row, 1.0).then_inc(ones_set, 1)

        @block.vector
        def _(dve):
            with taken(dve, whole, whole_ready, when):
                ln = [0]

                def link(ins):
                    ln[0] += 1
                    ins.then_inc(ln_step, 1)
                    dve.wait_ge(ln_step, ln[0])

                for c in range(CHUNKS):
                    dve.wait_ge(x_in[c], 16)
                    for i in range(PER):
                        last = nc.vector.bn_stats(stats[:, i, :], x_all[:, PER * c + i, :])
                    link(last)
                    for i in range(PER):
                        last = nc.vector.bn_aggr(moments[:, i, :], stats[:, i, :])
                    link(last)
                    nc.vector.tensor_scalar(spread[:, 0, :], moments[:, :, 1], LN_EPS, None, ALU.add).then_inc(variance_ready, 1)
                    dve.wait_ge(root_ready, c + 1)
                    link(nc.vector.reciprocal(spread[:, 2, :], spread[:, 1, :]))
                    link(nc.vector.tensor_tensor(spread[:, 2, :], spread[:, 2, :], spread[:, 0, :], ALU.mult))
                    link(nc.vector.tensor_tensor(spread[:, 2, :], spread[:, 2, :], spread[:, 1, :], ALU.add))
                    link(nc.vector.tensor_scalar(spread[:, 2, :], spread[:, 2, :], 0.5, None, ALU.mult))
                    link(nc.vector.reciprocal(spread[:, 1, :], spread[:, 2, :]))
                    if c:
                        dve.wait_ge(nodes_turned, c)
                    for i in range(PER):
                        last = nc.vector.tensor_scalar(node_major[:, i, :], x_all[:, PER * c + i, :], moments[:, i, 0:1],
                                                       spread[:, 1, i:i + 1], ALU.subtract, ALU.mult)
                    last.then_inc(nodes_ready, 1)
                    dve.wait_ge(nodes_ready, c + 1)

                def take_max(l, c, t):
                    g, par = l * CHUNKS + c, l % 2
                    if t == 0 and not (isinstance(g, int) and g == 0):
                        dve.wait_ge(largest_turned, g)
                    if t % PER == 0:
                        dve.wait_ge(al_scaled, CHUNKS * l + t // PER + 1)
                    if streamed:
                        dve.wait_ge(max_tile_in, 16 * (TILES * g + t) + 16)
                    code = max_tile[:, :] if streamed else counts[:, t, chunk_columns(c)]
                    if t == 0:
                        ins = nc.vector.tensor_scalar(largest[:, :], code, tile_column(al_tiny, par, t), None, ALU.min)
                    else:
                        dve.wait_ge(maxed, TILES * g + t)
                        ins = nc.vector.scalar_tensor_tensor(out=largest[:, :], in0=code, scalar=tile_column(al_tiny, par, t),
                                                             in1=largest[:, :], op0=ALU.min, op1=ALU.max)
                    ins.then_inc(maxed, 1)

                def columns(l, c):
                    g, par = l * CHUNKS + c, l % 2
                    first = isinstance(g, int) and g == 0
                    dve.wait_ge(largest_turned, g + 1)
                    nc.vector.tensor_reduce(out=peak[:, 0:4], in_=psum[0:LANES, START, 0:4 * LANES].rearrange("p (i s) -> p i s", s=LANES),
                                            axis=AX, op=ALU.max).then_inc(col_step, 1)
                    nc.vector.tensor_reduce(out=peak[:, 4:5], in_=psum[0:LANES, START + 1, 0:LANES],
                                            axis=AX, op=ALU.max).then_inc(col_step, 1)
                    al_d = one_of(al, par)[:, tile_range(c), 1]
                    if not first:
                        dve.wait_ge(rows_spread, 3 * g)
                    dve.wait_ge(col_step, 5 * g + 2)
                    nc.vector.tensor_scalar(row_cols[:, 0, :], peak[:, :], HUGE, None, ALU.mult).then_inc(col_step, 1)
                    dve.wait_ge(col_step, 5 * g + 3)
                    nc.vector.tensor_tensor(z_col[:, :], row_cols[:, 0, :], al_d, ALU.add).then_inc(col_step, 1)
                    dve.wait_ge(col_step, 5 * g + 4)
                    nc.vector.tensor_scalar(z_col[:, :], z_col[:, :], 0.0, (1 - SLOPE) / SLOPE, ALU.max, ALU.mult).then_inc(col_step, 1)
                    dve.wait_ge(col_step, 5 * g + 5)
                    nc.vector.tensor_tensor(z_col[:, :], z_col[:, :], row_cols[:, 0, :], ALU.add).then_inc(col_done, 1)
                    dve.wait_ge(col_done, g + 1)
                    nc.vector.tensor_scalar(row_cols[:, 1, :], z_col[:, :], SLOPE, None, ALU.mult).then_inc(cols_ready, 1)

                def exponent(l, c, t):
                    g, par = l * CHUNKS + c, l % 2
                    if t == 0:
                        dve.wait_ge(rows_ready, g + 1)
                    dve.wait_ge(distance_ready, TILES * g + t + 1)
                    slot = ring[0:LANES, t % RING, :]
                    nc.vector.scalar_tensor_tensor(out=slot, in0=one_of(rows, g % 2)[:, WIDE:2 * WIDE], scalar=tile_column(al_fifth, par, t),
                                                   in1=slot, op0=ALU.subtract, op1=ALU.min).then_inc(exponent_ready, 1)

                def weigh(l, c, t):
                    g = l * CHUNKS + c
                    dve.wait_ge(exp_ready, TILES * g + t + 1)
                    slot = ring[0:LANES, t % RING, :]
                    if streamed:
                        dve.wait_ge(weigh_tile_in, 16 * (TILES * g + t) + 16)
                    code = weigh_tile[:, :] if streamed else counts[:, t, chunk_columns(c)]
                    nc.vector.scalar_tensor_tensor(out=slot, in0=code, scalar=1.0, in1=slot,
                                                   op0=ALU.add, op1=ALU.mult).then_inc(weight_ready, 1)

                def denominators(g):
                    dve.wait_ge(tile_used, TILES * g + 2 * TILES)
                    dve.wait_ge(nodes_ready, g + CHUNKS)
                    for b, n in ((0, 3), (1, 2)):
                        last = nc.vector.tensor_scalar(
                            denom[:, 3 * b:3 * b + n],
                            psum[0:LANES, SUMS + b, 0:n * (FEAT + 1)].rearrange("p (i f) -> p i f", f=FEAT + 1)[:, :, FEAT],
                            2 * SOFTMAX_EPS, None, ALU.add)
                    last.then_inc(denom_step, 1)
                    dve.wait_ge(denom_step, g + 1)
                    nc.vector.reciprocal(denom[:, :], denom[:, :]).then_inc(denom_ready, 1)

                def add_x(c):
                    dve.wait_ge(sigmoid_ready, c + 1)
                    dve.wait_ge(x_again, 16 * c + 16)
                    nc.vector.tensor_tensor(result, result, x_chunk, ALU.add).then_inc(result_ready, 1)

                def step(l, c):
                    g = l * CHUNKS + c
                    last_layer = isinstance(l, int)
                    more = c < CHUNKS - 1
                    plan = max_plan(more, last_layer)
                    exponent(l, c, 0)
                    exponent(l, c, 1)
                    if c:
                        denominators(g - 1)
                    for t in range(TILES):
                        if t == AFTER + 1 and more:
                            columns(l, c + 1)
                        if t + 2 < TILES:
                            exponent(l, c, t + 2)
                        weigh(l, c, t)
                        for a in plan[t]:
                            take_max(*((l, c + 1) if more else (l + 1, 0)), a)
                        if last_layer and c and t == 10:
                            add_x(c - 1)
                    if not more:
                        denominators(g)
                        if last_layer:
                            add_x(c)
                        else:
                            for a in range(20, TILES):
                                take_max(l + 1, 0, a)
                            columns(l + 1, 0)

                for t in range(TILES):
                    take_max(0, 0, t)
                columns(0, 0)
                with dve.Fori(0, LAYERS - 1) as l:
                    for c in range(CHUNKS):
                        step(l, c)
                for c in range(CHUNKS):
                    step(LAYERS - 1, c)

        @block.tensor
        def _(pe):
            with taken(pe, whole, whole_ready, when):
                def turn_nodes(f):
                    pe.wait_ge(nodes_ready, f + 1)
                    for i in range(PER):
                        last = nc.tensor.transpose(piece(FINISH, i, 128), node_major[:, i, :], ident[0:LANES, 0:LANES])
                    last.then_inc(nodes_turned, 1)

                def dense(w, copied):
                    copied()
                    nc.tensor.matmul(psum[:, FINISH, 0:4 * LANES], w, feat_major[:, 0:4 * LANES], start=True, stop=True)
                    nc.tensor.matmul(psum[:, FINISH + 1, 0:LANES], w, feat_major[:, 4 * LANES:WIDE], start=True, stop=True).then_inc(dense_ready, 1)

                def make_hidden(f, k, first, frees_ring=False):
                    if first:
                        pe.wait_ge(weights_in, 32 * k + 32)
                    for i in range(PER):
                        at = (FEAT + 2) * (i % 3)
                        last = nc.tensor.matmul(psum[0:LANES, FINISH + i // 3, at:at + FEAT + 2], feat_major[:, LANES * i:LANES * (i + 1)],
                                                weights[:, :], start=True, stop=True)
                        if i == 0 and frees_ring:
                            last.then_inc(tile_used, TILES // CHUNKS)
                    last.then_inc(hidden_mm, 1)

                pe.wait_ge(consts_in, 64)
                for c in range(CHUNKS):
                    turn_nodes(c)
                    dense(enc_w[:, 0, :], lambda: pe.wait_ge(feats_ready, c + 1))
                    dense(enc_w[:, 1, :], lambda: pe.wait_ge(dense_copied, 3 * c + 1))
                    dense(enc_w[:, 2, :], lambda: pe.wait_ge(dense_copied, 3 * c + 2))
                    pe.wait_ge(dense_copied, 3 * c + 3)
                    make_hidden(c, 0, c == 0, frees_ring=True)
                    pe.wait_ge(hidden_ready, c + 1)

                def turn_largest(g):
                    pe.wait_ge(maxed, TILES * g + TILES)
                    if not (isinstance(g, int) and g == 0):
                        pe.wait_ge(rows_ready, g)
                    for i in range(PER):
                        last = nc.tensor.transpose(piece(START, i), largest[:, LANES * i:LANES * (i + 1)], ident[0:LANES, 0:LANES])
                    last.then_inc(largest_turned, 1)

                def spread_rows(g):
                    pe.wait_ge(cols_ready, g + 1)
                    for q in range(2 * PER):
                        last = nc.tensor.transpose(piece(START, q), row_cols[:, q // PER, q % PER:q % PER + 1].broadcast_to([LANES, LANES]),
                                                   ident[0:LANES, 0:LANES])
                        if q % PER_BANK == PER_BANK - 1 or q == 2 * PER - 1:
                            last.then_inc(rows_spread, 1)

                def add_tile(l, c, t):
                    g = l * CHUNKS + c
                    pe.wait_ge(weight_ready, TILES * g + t + 1)
                    if t == 0:
                        pe.wait_ge(nodes_ready, g + CHUNKS)
                    for i in range(PER):
                        last = nc.tensor.matmul(sums(i), ring[0:LANES, t % RING, LANES * i:LANES * (i + 1)],
                                                one_of(hidden[0:LANES], l % 2)[:, t, :], start=t == 0 and i % 3 == 0, stop=t == TILES - 1,
                                                skip_group_check=True)
                    last.then_inc(tile_used, 1)

                def finish_next(l, c):
                    f = (l + 1) * CHUNKS + c
                    yield lambda: turn_nodes(f)

                    def hid():
                        pe.wait_ge(feats_ready, f + 1)
                        make_hidden(f, l + 1, c == 0)
                    yield hid

                def finish_decoder(c):
                    f = LAYERS * CHUNKS + c
                    yield lambda: turn_nodes(f)

                    def first():
                        pe.wait_ge(dec_in, 32)
                        dense(dec_w[:, 0, :], lambda: pe.wait_ge(feats_ready, f + 1))
                    yield first
                    yield lambda: dense(dec_w[:, 1, :], lambda: pe.wait_ge(dense_copied, 3 * CHUNKS + 2 * c + 1))

                    def logits():
                        pe.wait_ge(dense_copied, 3 * CHUNKS + 2 * c + 2)
                        pe.wait_ge(ones_set, 3)
                        for i in range(PER):
                            at = psum[0:LANES, FINISH + i // 4, FEAT * (i % 4):FEAT * (i % 4 + 1)]
                            nc.tensor.matmul(at, feat_major[:, LANES * i:LANES * (i + 1)], dec_w[:, 2, :], start=i % 4 == 0, stop=False,
                                             skip_group_check=True)
                            last = nc.tensor.matmul(at, one_row, dec_row, start=False, stop=True, skip_group_check=True)
                        last.then_inc(hidden_mm, 1)
                    yield logits

                def step(l, c):
                    g = l * CHUNKS + c
                    last_layer = isinstance(l, int)
                    more = c < CHUNKS - 1
                    finish = lambda c: list(finish_decoder(c) if last_layer else finish_next(l, c))
                    before = finish(c - 1) if c else []
                    for t in range(TILES):
                        if t % 2 == 0 and t // 2 < len(before):
                            if t:
                                pass
                            before[t // 2]()
                        if t == AFTER and more:
                            turn_largest(g + 1)
                        if t == AFTER + 2 and more:
                            spread_rows(g + 1)
                        add_tile(l, c, t)
                    if not more:
                        for part in finish(c):
                            part()
                        if not last_layer:
                            turn_largest(g + 1)
                            spread_rows(g + 1)

                pe.wait_ge(ones_set, 2)
                turn_largest(0)
                spread_rows(0)
                with pe.Fori(0, LAYERS - 1) as l:
                    for c in range(CHUNKS):
                        step(l, c)
                for c in range(CHUNKS):
                    step(LAYERS - 1, c)

        @block.scalar
        def _(act):
            with taken(act, whole, whole_ready, when):
                def copy_feats(f, bias):
                    act.wait_ge(nodes_turned, f + 1)
                    nc.scalar.activation(feat_major[:, 0:4 * LANES], psum[:, FINISH, 0:4 * LANES], ACT.Relu, bias=bias)
                    nc.scalar.activation(feat_major[:, 4 * LANES:WIDE], psum[:, FINISH + 1, 0:LANES], ACT.Relu, bias=bias).then_inc(feats_ready, 1)

                def copy_dense(number, func, bias):
                    act.wait_ge(dense_ready, number + 1)
                    nc.scalar.activation(feat_major[:, 0:4 * LANES], psum[:, FINISH, 0:4 * LANES], func, bias=bias)
                    nc.scalar.activation(feat_major[:, 4 * LANES:WIDE], psum[:, FINISH + 1, 0:LANES], func, bias=bias).then_inc(dense_copied, 1)

                def copy_hidden(l, c, k):
                    f = k * CHUNKS + c
                    al_k, tiny_k, minus_k, fifth_k = (one_of(a, k % 2) for a in (al, al_tiny, al_minus, al_fifth))
                    hidden_k = one_of(hidden[0:LANES], k % 2)
                    act.wait_ge(hidden_mm, f + 1)
                    for i, n in ((0, 3), (1, 2)):
                        tiles = slice(PER * c + 3 * i, PER * c + 3 * i + n)
                        nc.scalar.activation(al_k[:, tiles, :], fresh(i, FEAT, FEAT + 2), ACT.Copy).then_inc(al_ready, 1)
                    for i, n in ((0, 3), (1, 2)):
                        tiles = slice(PER * c + 3 * i, PER * c + 3 * i + n)
                        last = nc.scalar.activation(hidden_k[:, tiles, 0:FEAT], fresh(i, 0, FEAT), ACT.Copy)
                    last.then_inc(hidden_ready, 1)
                    act.wait_ge(al_ready, 2 * f + 2)
                    own = slice(PER * c, PER * (c + 1))
                    nc.scalar.mul(tiny_k[:, own], al_k[:, own, 0], TINY)
                    nc.scalar.mul(minus_k[:, own], al_k[:, own, 0], -1.0)
                    nc.scalar.mul(fifth_k[:, own], al_k[:, own, 0], SLOPE).then_inc(al_scaled, 1)

                act.wait_ge(consts_in, 64)
                for c in range(CHUNKS):
                    act.wait_ge(variance_ready, c + 1)
                    nc.scalar.activation(spread[:, 1, :], spread[:, 0, :], ACT.Sqrt).then_inc(root_ready, 1)
                    copy_feats(c, 0.0)
                    for k, func in enumerate((ACT.Relu, ACT.Relu, ACT.Identity)):
                        copy_dense(3 * c + k, func, enc_bias[:, k:k + 1])
                    copy_hidden(None, c, 0)

                def copy_rows(g):
                    for b, n in enumerate((4, 4, 2)):
                        act.wait_ge(rows_spread, 3 * g + b + 1)
                        last = nc.scalar.activation(one_of(rows, g % 2)[:, 4 * LANES * b:4 * LANES * b + LANES * n],
                                                    psum[0:LANES, START + b, 0:LANES * n], ACT.Copy)
                    last.then_inc(rows_ready, 1)

                def distance(l, c, t):
                    g, par = l * CHUNKS + c, l % 2
                    act.wait_ge(tile_used, TILES * g + TILES + (t - RING + 1 if t >= RING else [0, -3, -2, -1][t]))
                    nc.scalar.activation(ring[0:LANES, t % RING, :], one_of(rows, g % 2)[:, 0:WIDE], ACT.Identity,
                                         bias=tile_column(al_minus, par, t)).then_inc(distance_ready, 1)

                def clamp(l, c, t):
                    g = l * CHUNKS + c
                    act.wait_ge(exponent_ready, TILES * g + t + 1)
                    slot = ring[0:LANES, t % RING, :]
                    nc.scalar.activation(slot, slot, ACT.Relu).then_inc(clamped, 1)

                def exp(l, c, t):
                    g = l * CHUNKS + c
                    act.wait_ge(clamped, TILES * g + t + 1)
                    slot = ring[0:LANES, t % RING, :]
                    nc.scalar.activation(slot, slot, ACT.Exp, scale=-1.0).then_inc(exp_ready, 1)

                def divide(g):
                    act.wait_ge(denom_ready, g + 1)
                    act.wait_ge(nodes_turned, g + CHUNKS)
                    for i in range(PER):
                        last = nc.scalar.activation(node_major[:, i, :], sums(i, 0, FEAT), ACT.Copy, scale=denom[:, i:i + 1])
                    last.then_inc(nodes_ready, 1)

                def finish_next(l, c):
                    yield lambda: divide(l * CHUNKS + c)
                    yield lambda: copy_feats((l + 1) * CHUNKS + c, conv_bias[:, bass.ds(l, 1)])
                    yield lambda: copy_hidden(l, c, l + 1)

                def finish_decoder(c):
                    l = LAYERS - 1
                    yield lambda: divide(l * CHUNKS + c)
                    yield lambda: copy_feats((l + 1) * CHUNKS + c, conv_bias[:, l:l + 1])
                    for k in range(2):
                        yield lambda k=k: copy_dense(3 * CHUNKS + 2 * c + k, ACT.Relu, dec_bias[:, k:k + 1])

                    def sigmoid():
                        act.wait_ge(hidden_mm, LAYERS * CHUNKS + c + 1)
                        act.wait_ge(dec_in, 32)
                        if c:
                            act.wait_ge(stored, 16 * c)
                        nc.scalar.activation(result[:, 0:4 * FEAT], psum[0:LANES, FINISH, 0:4 * FEAT], ACT.Sigmoid)
                        nc.scalar.activation(result[:, 4 * FEAT:5 * FEAT], psum[0:LANES, FINISH + 1, 0:FEAT], ACT.Sigmoid).then_inc(sigmoid_ready, 1)
                    yield sigmoid

                def step(l, c):
                    g = l * CHUNKS + c
                    last_layer = isinstance(l, int)
                    more = c < CHUNKS - 1
                    finish = lambda c: list(finish_decoder(c) if last_layer else finish_next(l, c))
                    before = finish(c - 1) if c else []
                    if not (isinstance(g, int) and g == 0):
                        act.wait_ge(rows_ready, g + 1)
                    for t in range(RING - 1):
                        distance(l, c, t)
                    clamp(l, c, 0)
                    for t in range(TILES):
                        if t + 1 < TILES:
                            clamp(l, c, t + 1)
                        exp(l, c, t)
                        if t + RING - 1 < TILES:
                            distance(l, c, t + RING - 1)
                        if t % 2 == 0 and t // 2 < len(before):
                            before[t // 2]()
                        if t == AFTER + 2 and more:
                            copy_rows(g + 1)
                    if not more:
                        for part in finish(c):
                            part()
                        if not last_layer:
                            copy_rows(g + 1)

                copy_rows(0)
                with act.Fori(0, LAYERS - 1) as l:
                    for c in range(CHUNKS):
                        step(l, c)
                for c in range(CHUNKS):
                    step(LAYERS - 1, c)


def one_of(buffers, n):
    if isinstance(n, int):
        return buffers[:, n]
    own = buffers[:, bass.ds(n, 1)]
    rest = " ".join("abcd"[:len(own.shape) - 2])
    return own.rearrange(f"p o {rest} -> p (o {rest[0]}) {rest[1:]}")


def tile_column(columns, par, t):
    return one_of(columns, par)[:, t:t + 1]


def tile_range(c):
    return slice(PER * c, PER * (c + 1))


def chunk_columns(c):
    return slice(WIDE * c, WIDE * (c + 1))


_INS = ["x", "src", "dst", "L0_gnn_enc_W", "L0_gnn_enc_b", "L0_gnn_conv_W", "L0_gnn_conv_att_src",
        "L0_gnn_conv_att_dst", "L0_gnn_conv_b", "L0_gnn_dec_W", "L0_gnn_dec_b"]


def kernel(**inputs):
    import numpy as _np
    import concourse.bacc as _bacc
    from concourse import mybir as _mybir
    from concourse.bass_utils import run_bass_kernel_spmd as _run

    nc = _bacc.Bacc("TRN2", target_bir_lowering=False, num_devices=1)
    arrays, args = {}, []
    for name in _INS:
        a = _np.ascontiguousarray(inputs[name])
        arrays[f"in_{name}"] = a
        args.append(nc.dram_tensor(f"in_{name}", a.shape, _mybir.dt.from_np(a.dtype), kind="ExternalInput").ap())
    args.append(nc.dram_tensor("out_0", (NODES, FEAT), F32, kind="ExternalOutput").ap())
    nc.disable_value_cache = True
    gat_program(nc, *args)
    r = _run(nc, [arrays], core_ids=[0])
    return r.results[0]["out_0"]
```

```python
import concourse.bass as bass
from concourse import mybir
from collections import namedtuple
from contextlib import ExitStack

F32 = mybir.dt.float32
I32 = mybir.dt.int32
U32 = mybir.dt.uint32
I16 = mybir.dt.int16
BF16 = mybir.dt.bfloat16
ALU = mybir.AluOpType
ACT = mybir.ActivationFunctionType
AX = mybir.AxisListType.X

NODES, FEAT, EDGES, LAYERS = 3125, 128, 53125, 9
SLOPE, LN_EPS, SOFTMAX_EPS = 0.2, 1e-5, 1e-16

LANES = 125
TILES = NODES // LANES
CHUNKS = 5
PER = TILES // CHUNKS
WIDE = PER * LANES

GRAIN = 25
ROWS = EDGES // GRAIN
ROWS_PER_LANE = ROWS // LANES
EDGES_PER_LANE = EDGES // LANES
BLOCK = 20
BLOCKS = -(-NODES // BLOCK)
LAST_BASE = NODES - BLOCK
LAST_NEW = NODES - BLOCK * (BLOCKS - 1)
HALF = 80
WINDOW = 512
FETCHED = WINDOW - BLOCK
PASSES = WINDOW // 128
CODES = BLOCK * TILES
SHIFT = 12
NOWHERE = (1 << SHIFT) - 1
RING = 4
LEAD = 3

SLOTS = TILES * CHUNKS

TINY = 2.0 ** -64
HUGE = 2.0 ** 64


def gat_program(nc, x, src, dst, enc_W, enc_b, conv_W, att_src, att_dst, conv_b, dec_W, dec_b, out):
    packed_d = nc.dram_tensor("packed_d", [EDGES + FETCHED], I32, kind="Internal").ap()
    firsts_d = nc.dram_tensor("firsts_d", [ROWS], F32, kind="Internal").ap()
    windows_d = nc.dram_tensor("windows_d", [ROWS, FETCHED], I32, kind="Internal").ap()
    counts_d = nc.dram_tensor("counts_d", [LANES, TILES, BLOCKS * BLOCK], F32, kind="Internal").ap()
    overlapping = bass.AP(tensor=packed_d.tensor, offset=0, ap=[[GRAIN, ROWS], [1, FETCHED]])

    top = ExitStack()
    with top:
        def sb(name, shape, dt=F32, stack=top):
            return stack.enter_context(nc.sbuf_tensor(name, shape, dt))

        def sem(name):
            return top.enter_context(nc.semaphore(name))

        ident = sb("ident", [128, 128])
        att_cols = sb("att_cols", [128, LAYERS, 2])
        whole = sb("whole", [1, 1], I32)
        whole_ready = sem("whole_ready")
        psum = top.enter_context(nc.psum_tensor("psum", [128, 8, 512], F32))

        resident = ExitStack()
        with resident:
            counts = sb("counts", [LANES, TILES, NODES], I16, resident)
            build_counts(nc, src, dst, conv_W, att_src, att_dst, packed_d, firsts_d, windows_d,
                         overlapping, counts, ident, att_cols, whole, whole_ready, psum, sem)
            network(nc, x, enc_W, enc_b, conv_W, conv_b, dec_W, dec_b, out, counts, None, ident, att_cols,
                    whole, whole_ready, psum, sem)

        build_counts_of_any(nc, src, dst, counts_d, whole, whole_ready, psum, lambda name: sem("any_" + name))
        network(nc, x, enc_W, enc_b, conv_W, conv_b, dec_W, dec_b, out, None, counts_d, ident, att_cols,
                whole, whole_ready, psum, lambda name: sem("any_" + name))


def taken(engine, whole, whole_ready, when):
    engine.wait_ge(whole_ready, 1)
    return engine.If(engine.value_load(whole[0:1, 0:1], min_val=0, max_val=1) == when)


def build_counts(nc, src, dst, conv_W, att_src, att_dst, packed_d, firsts_d, windows_d,
                 overlapping, counts, ident, att_cols, whole, whole_ready, psum, sem):
    scope = ExitStack()
    with scope:
        def sb(name, shape, dt=F32):
            return scope.enter_context(nc.sbuf_tensor(name, shape, dt))

        edges = sb("edges", [LANES, 2, EDGES_PER_LANE], I32)
        packed = sb("packed", [LANES, EDGES_PER_LANE], I32)
        firsts = sb("firsts", [LANES, ROWS_PER_LANE])
        beyond = sb("beyond", [1, FETCHED], I32)
        all_firsts = sb("all_firsts", [HALF, ROWS])
        below = sb("below", [HALF, ROWS], BF16)
        base_i = sb("base_i", [HALF, 2], I32)
        base = sb("base", [HALF, 2])
        rows_below = sb("rows_below", [HALF, 2])
        own_code = sb("own_code", [HALF, 2])
        held = sb("held", [HALF, 2])
        ones = sb("window_ones", [HALF, 1])
        first_row = sb("first_row", [HALF, 2], U32)
        window = sb("window", [HALF, 2, WINDOW], I32)
        src_f = sb("src_f", [HALF, 2 * WINDOW])
        wrong = code_f = src_f
        tile_i = sb("tile_i", [HALF, 2 * WINDOW], I32)
        tile_f = sb("tile_f", [HALF, 2 * WINDOW])
        lane_f = sb("lane_f", [HALF, 2 * WINDOW])
        lane_t = sb("lane_t", [128, PASSES, 2 * HALF])
        code_t = sb("code_t", [128, PASSES, 2 * HALF])
        iota_i = sb("iota_i", [128, CODES], I16)
        lane_hot = sb("lane_hot", [128, PASSES, LANES], BF16)
        code_hot = sb("code_hot", [128, PASSES, CODES], BF16)
        weights = sb("weights", [128, FEAT])
        att = sb("att", [128, 2, FEAT])
        product = sb("product", [128, FEAT])
        att_pair = sb("att_pair", [128, 2])

        edges_in = sem("edges_in")
        packed_out = sem("packed_out")
        windows_out = sem("windows_out")
        firsts_in = sem("firsts_in")
        weights_in = sem("weights_in")
        window_in = [sem("window_in0"), sem("window_in1")]
        pool_setup = sem("pool_setup")
        step = sem("dve_step")
        held_ready = sem("held_ready")
        held_summed = sem("held_summed")
        att_step = sem("att_step")
        packed_ready = sem("packed_ready")
        firsts_ready = sem("firsts_ready")
        first_row_ready = sem("first_row_ready")
        split_ready = sem("split_ready")
        turned = sem("turned")
        turned_copied = sem("turned_copied")
        hot_ready = sem("hot_ready")
        hot_used = sem("hot_used")
        block_stored = sem("block_stored")
        block = scope.enter_context(nc.Block())

        @block.sync
        def _(sp):
            sp.dma_start(edges[:, 1, :], dst.rearrange("(p j) -> p j", p=LANES)).then_inc(edges_in, 16)
            sp.dma_start(edges[:, 0, :], src.rearrange("(p j) -> p j", p=LANES)).then_inc(edges_in, 16)
            sp.wait_ge(firsts_ready, 1)
            sp.dma_start(firsts_d.rearrange("(p j) -> p j", p=LANES), firsts[:, :]).then_inc(firsts_in, 16)
            sp.wait_ge(packed_ready, 1)
            sp.wait_ge(pool_setup, 2)
            sp.dma_start(packed_d[0:EDGES].rearrange("(p j) -> p j", p=LANES), packed[:, :]).then_inc(packed_out, 16)
            sp.dma_start(packed_d[EDGES:EDGES + FETCHED].rearrange("(a j) -> a j", a=1), beyond[:, :]).then_inc(packed_out, 16)
            sp.wait_ge(firsts_in, 16)
            sp.dma_start(all_firsts[:, :], firsts_d.rearrange("(a j) -> a j", a=1).broadcast_to([HALF, ROWS])).then_inc(firsts_in, 16)
            sp.wait_ge(packed_out, 32)
            sp.dma_start(windows_d[:, :], overlapping).then_inc(windows_out, 16)
            with sp.Fori(0, LAYERS) as l:
                sp.wait_ge(att_step, 3 * l + 1)
                sp.dma_start(weights[:, :], conv_W[bass.ds(l, 1), :, :].rearrange("l k n -> (l k) n")).then_inc(weights_in, 16)
                sp.dma_start(att[:, 0, :], att_src[bass.ds(l, 1), :].broadcast_to([128, FEAT])).then_inc(weights_in, 16)
                sp.dma_start(att[:, 1, :], att_dst[bass.ds(l, 1), :].broadcast_to([128, FEAT])).then_inc(weights_in, 16)
            sp.wait_ge(weights_in, 48 * LAYERS)

        @block.gpsimd
        def _(pool):
            nc.gpsimd.iota(base_i[:, :], [[BLOCK * HALF, 2]], base=0, channel_multiplier=BLOCK).then_inc(pool_setup, 1)
            nc.gpsimd.memset(beyond[:, :], NOWHERE << SHIFT).then_inc(pool_setup, 1)
            nc.gpsimd.iota(iota_i[:, :], [[1, CODES]], base=0, channel_multiplier=0,
                           allow_small_or_imprecise_dtypes=True).then_inc(pool_setup, 1)
            nc.gpsimd.memset(ident[:, :], 0.0).then_inc(pool_setup, 1)
            pool.wait_ge(pool_setup, 4)
            nc.gpsimd.affine_select(out=ident[:, :], in_=ident[:, :], compare_op=ALU.not_equal, fill=1.0,
                                    base=0, pattern=[[-1, 128]], channel_multiplier=1).then_inc(pool_setup, 1)
            both = (1 << SHIFT) + 1
            for k in range(2):
                nc.gpsimd.iota(window[:, k, FETCHED:WINDOW], [[both, BLOCK]], base=BLOCK * HALF * k * both,
                               channel_multiplier=BLOCK * both).then_inc(pool_setup, 1)
            pool.wait_ge(first_row_ready, 1)
            pool.wait_ge(windows_out, 16)
            for k in range(2):
                nc.gpsimd.indirect_dma_start(
                    out=window[:, k, 0:FETCHED], out_offset=None, in_=windows_d[:, :],
                    in_offset=bass.IndirectOffsetOnAxis(ap=first_row[:, k:k + 1], axis=0)).then_inc(window_in[k], 16)
            for k in range(2):
                pool.wait_ge(window_in[k], 16)

        @block.vector
        def _(dve):
            done = [0]

            def link(ins):
                done[0] += 1
                ins.then_inc(step, 1)
                dve.wait_ge(step, done[0])

            dve.wait_ge(edges_in, 32)
            nc.vector.tensor_copy(firsts[:, :], edges[:, 1, :].rearrange("p (r g) -> p r g", g=GRAIN)[:, :, 0]).then_inc(firsts_ready, 1)
            nc.vector.scalar_tensor_tensor(out=packed[:, :], in0=edges[:, 1, :], scalar=float(1 << SHIFT), in1=edges[:, 0, :],
                                           op0=ALU.mult, op1=ALU.add).then_inc(packed_ready, 1)
            dve.wait_ge(pool_setup, 1)
            link(nc.vector.tensor_copy(base[:, :], base_i[:, :]))
            link(nc.vector.tensor_scalar(own_code[:, :], base[:, :], float(LAST_BASE), 0.0, ALU.subtract, ALU.max))
            link(nc.vector.tensor_scalar(own_code[:, :], own_code[:, :], float(TILES), None, ALU.mult))
            link(nc.vector.tensor_scalar(base[:, :], base[:, :], float(LAST_BASE), None, ALU.min))
            dve.wait_ge(firsts_in, 32)
            for k in range(2):
                link(nc.vector.tensor_scalar(below[:, :], all_firsts[:, :], base[:, k:k + 1], None, ALU.is_lt, ALU.add,
                                             accum_out=rows_below[:, k:k + 1]))
            nc.vector.tensor_scalar(first_row[:, :], rows_below[:, :], -1.0, 0.0, ALU.add, ALU.max).then_inc(first_row_ready, 1)

            dve.wait_ge(step, done[0])
            nc.vector.memset(product[:, :], 0.0).then_inc(att_step, 1)
            dve.wait_ge(att_step, 1)
            with dve.Fori(0, LAYERS) as l:
                dve.wait_ge(weights_in, 48 * l + 48)
                for k in range(2):
                    nc.vector.tensor_tensor_reduce(out=product[:, :], in0=weights[:, :], in1=att[:, k, :], scale=1.0, scalar=0.0,
                                                   op0=ALU.mult, op1=ALU.add,
                                                   accum_out=att_pair[:, k:k + 1]).then_inc(att_step, 1)
                    dve.wait_ge(att_step, 3 * l + 2 + k)
                nc.vector.tensor_copy(att_cols[:, bass.ds(l, 1), :].rearrange("p l a -> p (l a)"), att_pair[:, :]).then_inc(att_step, 1)
                dve.wait_ge(att_step, 3 * l + 4)

            for k in range(2):
                dve.wait_ge(window_in[k], 16)
            dve.wait_ge(pool_setup, 7)
            flat = window[:, :, :].rearrange("p k w -> p (k w)")
            link(nc.vector.tensor_scalar(tile_i[:, :], flat, NOWHERE, None, ALU.bitwise_and))
            link(nc.vector.tensor_copy(src_f[:, :], tile_i[:, :]))
            link(nc.vector.tensor_scalar(tile_i[:, :], src_f[:, :], 0.5, 1.0 / LANES, ALU.add, ALU.mult))
            link(nc.vector.tensor_copy(tile_f[:, :], tile_i[:, :]))
            link(nc.vector.scalar_tensor_tensor(out=lane_f[:, :], in0=tile_f[:, :], scalar=-float(LANES), in1=src_f[:, :], op0=ALU.mult, op1=ALU.add))
            link(nc.vector.tensor_scalar(wrong[:, :], lane_f[:, :], 0.0, None, ALU.is_lt))
            link(nc.vector.tensor_tensor(tile_f[:, :], tile_f[:, :], wrong[:, :], ALU.subtract))
            nc.vector.scalar_tensor_tensor(out=lane_f[:, :], in0=wrong[:, :], scalar=float(LANES), in1=lane_f[:, :], op0=ALU.mult, op1=ALU.add).then_inc(split_ready, 1)
            dve.wait_ge(split_ready, 1)
            link(nc.vector.tensor_scalar(tile_i[:, :], flat, SHIFT, None, ALU.logical_shift_right))
            for k in range(2):
                half = slice(WINDOW * k, WINDOW * (k + 1))
                link(nc.vector.tensor_scalar(code_f[:, half], tile_i[:, half], base[:, k:k + 1], float(TILES), ALU.subtract, ALU.mult))
            nc.vector.tensor_tensor(code_f[:, :], code_f[:, :], tile_f[:, :], ALU.add).then_inc(split_ready, 1)

            dve.wait_ge(split_ready, 2)
            link(nc.vector.memset(ones[:, :], 1.0))
            for k in range(2):
                half = slice(WINDOW * k, WINDOW * (k + 1))
                link(nc.vector.tensor_scalar(tile_f[:, half], code_f[:, half], own_code[:, k:k + 1], None, ALU.is_ge))
                link(nc.vector.scalar_tensor_tensor(out=tile_f[:, half], in0=code_f[:, half], scalar=float(CODES), in1=tile_f[:, half],
                                                    op0=ALU.is_lt, op1=ALU.mult))
            nc.vector.tensor_reduce(out=held[:, :], in_=tile_f[:, :].rearrange("p (k w) -> p k w", k=2), axis=AX,
                                    op=ALU.add).then_inc(held_ready, 1)
            dve.wait_ge(held_summed, 1)
            link(nc.vector.tensor_reduce(out=held[0:1, 0:1], in_=psum[0:1, 6, 0:2], axis=AX, op=ALU.add))
            nc.vector.tensor_scalar(whole[:, :], held[0:1, 0:1], float(EDGES + NODES), None, ALU.is_equal).then_inc(whole_ready, 1)

            dve.wait_ge(turned_copied, 2)

            def one_hots(b, first=False):
                for j in range(PASSES):
                    if not first:
                        dve.wait_ge(hot_used, PASSES * b - PASSES + j + 1)
                    at = slice(b, b + 1) if isinstance(b, int) else bass.ds(b, 1)
                    nc.vector.tensor_scalar(lane_hot[:, j, :], iota_i[:, 0:LANES], lane_t[:, j, at], None, ALU.is_equal).then_inc(hot_ready, 1)
                    nc.vector.tensor_scalar(code_hot[:, j, :], iota_i[:, :], code_t[:, j, at], None, ALU.is_equal).then_inc(hot_ready, 1)

            one_hots(0, first=True)
            with dve.Fori(1, BLOCKS) as b:
                one_hots(b)

        @block.tensor
        def _(pe):
            pe.wait_ge(pool_setup, 5)
            for n, part in enumerate((lane_f, code_f)):
                pe.wait_ge(split_ready, n + 1)
                for j in range(PASSES):
                    for k in range(2):
                        at = WINDOW * k + 128 * j
                        last = nc.tensor.transpose(psum[:, 2 * n + j // 2, 256 * (j % 2) + HALF * k:256 * (j % 2) + HALF * (k + 1)],
                                                   part[:, at:at + 128], ident[0:HALF, 0:HALF])
                last.then_inc(turned, 1)
            pe.wait_ge(held_ready, 1)
            nc.tensor.matmul(psum[0:1, 6, 0:2], ones[:, :], held[:, :], start=True, stop=True).then_inc(held_summed, 1)

            def count(b, bank):
                for j in range(PASSES):
                    pe.wait_ge(hot_ready, 2 * PASSES * b + 2 * j + 2)
                    last = nc.tensor.matmul(psum[0:LANES, bank, 0:CODES], lane_hot[:, j, :], code_hot[:, j, :],
                                            start=j == 0, stop=j == PASSES - 1)
                    last.then_inc(hot_used, 1)

            count(0, 4)
            count(1, 5)
            with pe.Fori(1, (BLOCKS - 1) // 2) as pair:
                for odd in range(2):
                    pe.wait_ge(block_stored, 2 * pair - 1 + odd)
                    count(2 * pair + odd, 4 + odd)
            pe.wait_ge(block_stored, BLOCKS - 2)
            count(BLOCKS - 1, 4)

        @block.scalar
        def _(act):
            for n, part in enumerate((lane_t, code_t)):
                act.wait_ge(turned, n + 1)
                nc.scalar.activation(part[:, :, :].rearrange("p (a b) c -> p a b c", a=2),
                                     psum[:, 2 * n:2 * n + 2, :].rearrange("p a (b c) -> p a b c", b=2)[:, :, :, 0:2 * HALF],
                                     ACT.Copy).then_inc(turned_copied, 1)

            def store(bank, at, first_dst, dsts, number):
                act.wait_ge(hot_used, number * PASSES)
                nc.scalar.activation(counts[:, :, at].rearrange("p t i -> p i t"),
                                     psum[0:LANES, bank, first_dst * TILES:(first_dst + dsts) * TILES].rearrange("p (i t) -> p i t", t=TILES),
                                     ACT.Copy, scale=2.0, bias=-1.0).then_inc(block_stored, 1)

            with act.Fori(0, (BLOCKS - 1) // 2) as pair:
                for odd in range(2):
                    store(4 + odd, bass.ds(2 * BLOCK * pair + BLOCK * odd, BLOCK), 0, BLOCK, 2 * pair + odd + 1)
            store(4, slice(NODES - LAST_NEW, NODES), BLOCK - LAST_NEW, LAST_NEW, BLOCKS)


def build_counts_of_any(nc, src, dst, counts_d, whole, whole_ready, psum, sem):
    scope = ExitStack()
    with scope:
        def sb(name, shape, dt=F32):
            return scope.enter_context(nc.sbuf_tensor("any_" + name, shape, dt))

        COLUMNS = EDGES_PER_LANE + TILES
        src_i = sb("src_i", [LANES, COLUMNS], I32)
        dst_i = sb("dst_i", [LANES, COLUMNS], I32)
        tile_i = sb("tile_i", [LANES, COLUMNS], I32)
        src_f = sb("src_f", [LANES, COLUMNS])
        wrong = src_f
        tile_f = sb("tile_f", [LANES, COLUMNS])
        lane_f = sb("lane_f", [LANES, COLUMNS])
        code_f = sb("code_f", [LANES, COLUMNS])
        iota_i = sb("iota_i", [LANES, CODES], I16)
        lane_hot = sb("lane_hot", [LANES, LANES], BF16)
        code_hot = sb("code_hot", [LANES, CODES], BF16)
        block_counts = sb("block_counts", [LANES, TILES, BLOCK])

        edges_in = sem("edges_in")
        loops_set = sem("loops_set")
        step = sem("dve_step")
        hot_ready = sem("hot_ready")
        hot_used = sem("hot_used")
        block_copied = sem("block_copied")
        block_stored = sem("block_stored")
        block = scope.enter_context(nc.Block())

        @block.sync
        def _(sp):
            with taken(sp, whole, whole_ready, 0):
                sp.dma_start(dst_i[:, 0:EDGES_PER_LANE], dst.rearrange("(p j) -> p j", p=LANES)).then_inc(edges_in, 16)
                sp.dma_start(src_i[:, 0:EDGES_PER_LANE], src.rearrange("(p j) -> p j", p=LANES)).then_inc(edges_in, 16)
                with sp.Fori(0, BLOCKS) as b:
                    sp.wait_ge(block_copied, b + 1)
                    sp.dma_start(counts_d[:, :, bass.ds(BLOCK * b, BLOCK)], block_counts[:, :, :]).then_inc(block_stored, 16)
                sp.wait_ge(block_stored, 16 * BLOCKS)

        @block.gpsimd
        def _(pool):
            with taken(pool, whole, whole_ready, 0):
                for ends in (src_i, dst_i):
                    nc.gpsimd.iota(ends[:, EDGES_PER_LANE:COLUMNS], [[LANES, TILES]], base=0, channel_multiplier=1).then_inc(loops_set, 1)
                nc.gpsimd.iota(iota_i[:, :], [[1, CODES]], base=0, channel_multiplier=0,
                               allow_small_or_imprecise_dtypes=True).then_inc(loops_set, 1)

        @block.vector
        def _(dve):
            with taken(dve, whole, whole_ready, 0):
                done = [0]

                def link(ins):
                    done[0] += 1
                    ins.then_inc(step, 1)
                    dve.wait_ge(step, done[0])

                dve.wait_ge(edges_in, 32)
                dve.wait_ge(loops_set, 3)
                link(nc.vector.tensor_copy(src_f[:, :], src_i[:, :]))
                link(nc.vector.tensor_copy(code_f[:, :], dst_i[:, :]))
                link(nc.vector.tensor_scalar(tile_i[:, :], src_f[:, :], 0.5, 1.0 / LANES, ALU.add, ALU.mult))
                link(nc.vector.tensor_copy(tile_f[:, :], tile_i[:, :]))
                link(nc.vector.scalar_tensor_tensor(out=lane_f[:, :], in0=tile_f[:, :], scalar=-float(LANES), in1=src_f[:, :], op0=ALU.mult, op1=ALU.add))
                link(nc.vector.tensor_scalar(wrong[:, :], lane_f[:, :], 0.0, None, ALU.is_lt))
                link(nc.vector.tensor_tensor(tile_f[:, :], tile_f[:, :], wrong[:, :], ALU.subtract))
                link(nc.vector.scalar_tensor_tensor(out=lane_f[:, :], in0=wrong[:, :], scalar=float(LANES), in1=lane_f[:, :], op0=ALU.mult, op1=ALU.add))
                link(nc.vector.scalar_tensor_tensor(out=code_f[:, :], in0=code_f[:, :], scalar=float(TILES), in1=tile_f[:, :], op0=ALU.mult, op1=ALU.add))

                def one_hots(j):
                    at = slice(j, j + 1) if isinstance(j, int) else bass.ds(j, 1)
                    nc.vector.tensor_scalar(lane_hot[:, :], iota_i[:, 0:LANES], lane_f[:, at], None, ALU.is_equal).then_inc(hot_ready, 1)
                    nc.vector.tensor_scalar(code_hot[:, :], iota_i[:, :], code_f[:, at], None, ALU.is_equal).then_inc(hot_ready, 1)

                def one_block(b):
                    if not isinstance(b, int):
                        dve.wait_ge(hot_used, COLUMNS * b)
                        nc.vector.tensor_scalar(code_f[:, :], code_f[:, :], float(CODES), None, ALU.subtract).then_inc(step, 1)
                        dve.wait_ge(step, b + done[0])
                    one_hots(0)
                    with dve.Fori(1, COLUMNS) as j:
                        dve.wait_ge(hot_used, COLUMNS * b + j)
                        one_hots(j)

                one_block(0)
                with dve.Fori(1, BLOCKS) as b:
                    one_block(b)

        @block.tensor
        def _(pe):
            def add_column(b, j):
                pe.wait_ge(hot_ready, 2 * (COLUMNS * b + j) + 2)
                fixed = isinstance(j, int)
                nc.tensor.matmul(psum[0:LANES, 4, 0:CODES], lane_hot[:, :], code_hot[:, :], start=fixed and j == 0,
                                 stop=fixed and j > 0, skip_group_check=True).then_inc(hot_used, 1)

            def one_block(b):
                if not isinstance(b, int):
                    pe.wait_ge(block_copied, b)
                add_column(b, 0)
                with pe.Fori(1, COLUMNS - 1) as j:
                    add_column(b, j)
                add_column(b, COLUMNS - 1)

            with taken(pe, whole, whole_ready, 0):
                one_block(0)
                with pe.Fori(1, BLOCKS) as b:
                    one_block(b)

        @block.scalar
        def _(act):
            def one_block(b):
                act.wait_ge(hot_used, COLUMNS * b + COLUMNS)
                if not isinstance(b, int):
                    act.wait_ge(block_stored, 16 * b)
                nc.scalar.activation(block_counts[:, :, :].rearrange("p t i -> p i t"),
                                     psum[0:LANES, 4, 0:CODES].rearrange("p (i t) -> p i t", t=TILES),
                                     ACT.Copy, scale=2.0, bias=-1.0).then_inc(block_copied, 1)

            with taken(act, whole, whole_ready, 0):
                one_block(0)
                with act.Fori(1, BLOCKS) as b:
                    one_block(b)


def network(nc, x, enc_W, enc_b, conv_W, conv_b, dec_W, dec_b, out, counts, counts_d, ident, att_cols,
            whole, whole_ready, psum, sem):
    scope = ExitStack()
    with scope:
        streamed = counts is None
        when = 0 if streamed else 1

        def sb(name, shape, dt=F32):
            return scope.enter_context(nc.sbuf_tensor("any_" + name if streamed else name, shape, dt))

        hidden = sb("hidden", [128, 2, TILES, FEAT + 1])
        al = sb("al", [LANES, 2, TILES, 2])
        al_tiny = sb("al_tiny", [LANES, 2, TILES])
        al_minus = sb("al_minus", [LANES, 2, TILES])
        al_fifth = sb("al_fifth", [LANES, 2, TILES])
        ring = sb("ring", [128, RING, WIDE])
        top_row = sb("top_row", [LANES, WIDE])
        bent_row = sb("bent_row", [LANES, 2, WIDE])
        largest = sb("largest", [LANES, 2, WIDE])
        node_major = sb("node_major", [LANES, PER, FEAT])
        feat_major = sb("feat_major", [128, WIDE])
        weights = sb("layer_weights", [128, FEAT + 2])
        peak = sb("peak", [LANES, PER])
        z_col = sb("z_col", [LANES, PER])
        row_cols = sb("row_cols", [LANES, 2, PER])
        denom = sb("denom", [LANES, PER])
        conv_bias = sb("conv_bias", [128, LAYERS])
        enc_bias = sb("enc_bias", [128, 3])
        dec_bias = sb("dec_bias", [128, 3])
        stats = sb("stats", [LANES, PER, 6])
        moments = sb("moments", [LANES, PER, 2])
        spread = sb("spread", [LANES, 3, PER])

        enc_w = ring[:, 0, 0:3 * FEAT].rearrange("p (k n) -> p k n", k=3)
        x_all = hidden[0:LANES, 1, :, 0:FEAT]
        spare = hidden[:, LAYERS % 2, :, :].rearrange("p t f -> p (t f)")
        dec_w = spare[:, 0:3 * FEAT].rearrange("p (k n) -> p k n", k=3)
        x_chunk = spare[0:LANES, 384:384 + PER * FEAT]
        result = spare[0:LANES, 1024:1024 + PER * FEAT]
        dec_row = spare[0:1, 1664:1664 + FEAT]
        one_row = spare[0:1, 1800:1800 + LANES]

        if streamed:
            max_tile = sb("max_tile", [LANES, WIDE])
            weigh_tile = sb("weigh_tile", [LANES, WIDE])
            max_tile_in = sem("max_tile_in")
            weigh_tile_in = sem("weigh_tile_in")

        consts_in = sem("consts_in")
        x_in = [sem(f"x_in{c}") for c in range(CHUNKS)]
        weights_in = sem("layer_weights_in")
        dec_in = sem("dec_in")
        x_again = sem("x_again")
        stored = sem("stored")
        ones_set = sem("ones_set")
        ln_step = sem("ln_step")
        variance_ready = sem("variance_ready")
        root_ready = sem("root_ready")
        nodes_ready = sem("nodes_ready")
        nodes_turned = sem("nodes_turned")
        feats_ready = sem("feats_ready")
        dense_ready = sem("dense_ready")
        dense_copied = sem("dense_copied")
        hidden_mm = sem("hidden_mm")
        hidden_ready = sem("hidden_ready")
        al_ready = sem("al_ready")
        al_scaled = sem("al_scaled")
        maxed = [sem("maxed_even"), sem("maxed_odd")]
        largest_turned = sem("largest_turned")
        col_step = sem("col_step")
        col_done = sem("col_done")
        cols_ready = sem("cols_ready")
        rows_spread = sem("rows_spread")
        rows_ready = sem("rows_ready")
        distance_ready = sem("distance_ready")
        exponent_ready = sem("exponent_ready")
        clamped = sem("clamped")
        exp_ready = sem("exp_ready")
        weight_ready = sem("weight_ready")
        tile_used = sem("tile_used")
        denom_step = sem("denom_step")
        denom_ready = sem("denom_ready")
        sigmoid_ready = sem("sigmoid_ready")
        result_ready = sem("result_ready")
        block = scope.enter_context(nc.Block())

        SUMS, FINISH, START = 0, 4, 5
        PER_BANK = 512 // LANES

        def piece(bank, i, n=LANES):
            return psum[0:n, bank + i // PER_BANK, LANES * (i % PER_BANK):LANES * (i % PER_BANK) + LANES]

        def sums(even_odd, i, a=0, b=FEAT + 1):
            at = (FEAT + 1) * (i % 3)
            return psum[0:LANES, SUMS + 2 * even_odd + i // 3, at + a:at + b]

        def fresh(i, a, b):
            n = 3 - i
            return psum[0:LANES, FINISH + i, 0:n * (FEAT + 2)].rearrange("p (t f) -> p t f", f=FEAT + 2)[:, :, a:b]

        HELD_BACK = PER
        EARLY = TILES - HELD_BACK

        def maxima(ahead, c, first=0, end=TILES):
            return [(ahead, c, t) for t in range(first, end)]

        def in_slots(last_layer):
            own = maxima(0, 1, EARLY) + maxima(0, 2) + maxima(0, 3) + maxima(0, 4)
            done = TILES * (CHUNKS - 1) - 10
            slots = [[] for _ in range(SLOTS)]
            for k, m in enumerate(own):
                slots[k * done // len(own)].append(m)
            if not last_layer:
                for k, m in enumerate(maxima(1, 0, 0, EARLY)):
                    slots[done + k * (SLOTS - 1 - done) // EARLY].append(m)
            return slots

        AT_END = [maxima(1, 1, 0, 2), maxima(1, 1, 2, 11), maxima(1, 0, EARLY), maxima(1, 1, 11, 14), maxima(1, 1, 14, EARLY)]
        BEFORE_LAYERS = [m for c in range(CHUNKS) for to in (0, 1) for m in maxima(0, to, PER * c, PER * c + PER) if (to, c) != (1, CHUNKS - 1)]

        DENOMINATORS, ADD_X = 0, 15
        NEXT_PE, NEXT_ACT = (6, 9), (1, 2, 3, 4, 5, 7, 8, 10, 11, 13)
        DECODER_PE, DECODER_ACT = (4, 7, 10, 13), (1, 1, 2, 2, 3, 5, 5, 8, 8, 11, 11, 14, 14)
        TURN_MAX, COLUMNS, SPREAD, ROWS = 15, 16, 18, TILES - 1 - LEAD
        def maxed_at(l, m):
            ahead, c, t = m
            k = following(l) if ahead else l
            return maxed[parity(k, c)], TILES * alike_before(k, c) + t + 1

        node_rows = lambda c: slice(c * WIDE, (c + 1) * WIDE)

        @block.sync
        def _(sp):
            with taken(sp, whole, whole_ready, when):
                for c in range(CHUNKS):
                    sp.dma_start(x_all[:, PER * c:PER * (c + 1), :],
                                 x[node_rows(c), :].rearrange("(t p) f -> p t f", p=LANES)).then_inc(x_in[c], 16)
                sp.dma_start(enc_w, enc_W.rearrange("k i n -> i k n")).then_inc(consts_in, 16)
                sp.dma_start(enc_bias[:, :], enc_b.rearrange("k f -> f k"), allow_slow_non_contiguous=True).then_inc(consts_in, 16)
                sp.dma_start(dec_bias[:, :], dec_b.rearrange("k f -> f k"), allow_slow_non_contiguous=True).then_inc(consts_in, 16)
                sp.dma_start(conv_bias[:, :], conv_b.rearrange("k f -> f k"), allow_slow_non_contiguous=True).then_inc(consts_in, 16)

                def load_tile(tile, loaded, used, count, c, t):
                    sp.wait_ge(used, count)
                    sp.dma_start(tile[:, :], counts_d[:, t, chunk_columns(c)]).then_inc(loaded, 16)

                def load_maxima(l, these, before):
                    for m in these:
                        used, count = maxed_at(l, before) if before else (ones_set, 1)
                        load_tile(max_tile, max_tile_in, used, count, m[1], m[2])
                        before = m
                    return before

                def stream_layer(l):
                    last_layer = isinstance(l.number, int)
                    before = (0, 1, EARLY - 1)
                    for slot, these in enumerate(in_slots(last_layer)):
                        before = load_maxima(l, these, before)
                        load_tile(weigh_tile, weigh_tile_in, tile_used, TILES + SLOTS * l.number + slot, *divmod(slot, TILES))
                        if last_layer and slot % TILES == TILES - 1:
                            c = slot // TILES
                            if c:
                                store_result(c - 1)
                            load_x(c)
                    if not last_layer:
                        load_maxima(l, sum(AT_END, []), before)

                def load_weights(k):
                    at = slice(k, k + 1) if isinstance(k, int) else bass.ds(k, 1)
                    sp.dma_start(weights[:, 0:FEAT], conv_W[at, :, :].rearrange("l k n -> (l k) n")).then_inc(weights_in, 16)
                    sp.dma_start(weights[:, FEAT:FEAT + 2], att_cols[:, at, :].rearrange("p l a -> p (l a)")).then_inc(weights_in, 16)

                def load_x(c):
                    sp.dma_start(x_chunk.rearrange("p (t f) -> p t f", f=FEAT),
                                 x[node_rows(c), :].rearrange("(t p) f -> p t f", p=LANES)).then_inc(x_again, 16)

                def store_result(c):
                    sp.wait_ge(result_ready, c + 1)
                    sp.dma_start(out[node_rows(c), :].rearrange("(t p) f -> p t f", p=LANES),
                                 result.rearrange("p (t f) -> p t f", f=FEAT)).then_inc(stored, 16)

                load_weights(0)
                if streamed:
                    load_maxima(FIRST, BEFORE_LAYERS, None)
                with sp.Fori(0, LAYERS // 2) as pair:
                    for second in range(2):
                        l = Layer(2 * pair + second, second, pair)
                        sp.wait_ge(hidden_mm, CHUNKS * l.number + CHUNKS)
                        load_weights(l.number + 1)
                        if streamed:
                            stream_layer(l)
                sp.wait_ge(tile_used, SLOTS * (LAYERS - 1) + TILES)
                sp.wait_ge(hidden_ready, CHUNKS * LAYERS)
                sp.dma_start(dec_w, dec_W.rearrange("k i n -> i k n")).then_inc(dec_in, 16)
                sp.dma_start(dec_row, dec_b[2:3, :]).then_inc(dec_in, 16)
                if streamed:
                    stream_layer(LAST)
                else:
                    load_x(0)
                    for c in range(1, CHUNKS):
                        store_result(c - 1)
                        load_x(c)
                store_result(CHUNKS - 1)
                sp.wait_ge(stored, 16 * CHUNKS)

        @block.gpsimd
        def _(pool):
            with taken(pool, whole, whole_ready, when):
                nc.gpsimd.memset(hidden[:, 0, :, FEAT:FEAT + 1], 1.0).then_inc(ones_set, 1)
                nc.gpsimd.memset(hidden[:, 1, :, FEAT:FEAT + 1], 1.0).then_inc(ones_set, 1)
                pool.wait_ge(tile_used, SLOTS * (LAYERS - 1) + TILES)
                nc.gpsimd.memset(one_row, 1.0).then_inc(ones_set, 1)

        @block.vector
        def _(dve):
            with taken(dve, whole, whole_ready, when):
                ln = [0]

                def link(ins):
                    ln[0] += 1
                    ins.then_inc(ln_step, 1)
                    dve.wait_ge(ln_step, ln[0])

                def normalise(c):
                    dve.wait_ge(x_in[c], 16)
                    for i in range(PER):
                        last = nc.vector.bn_stats(stats[:, i, :], x_all[:, PER * c + i, :])
                    link(last)
                    for i in range(PER):
                        last = nc.vector.bn_aggr(moments[:, i, :], stats[:, i, :])
                    link(last)
                    nc.vector.tensor_scalar(spread[:, 0, :], moments[:, :, 1], LN_EPS, None, ALU.add).then_inc(variance_ready, 1)
                    dve.wait_ge(root_ready, c + 1)
                    link(nc.vector.reciprocal(spread[:, 2, :], spread[:, 1, :]))
                    link(nc.vector.tensor_tensor(spread[:, 2, :], spread[:, 2, :], spread[:, 0, :], ALU.mult))
                    link(nc.vector.tensor_tensor(spread[:, 2, :], spread[:, 2, :], spread[:, 1, :], ALU.add))
                    link(nc.vector.tensor_scalar(spread[:, 2, :], spread[:, 2, :], 0.5, None, ALU.mult))
                    link(nc.vector.reciprocal(spread[:, 1, :], spread[:, 2, :]))
                    if c:
                        dve.wait_ge(nodes_turned, c)
                    for i in range(PER):
                        last = nc.vector.tensor_scalar(node_major[:, i, :], x_all[:, PER * c + i, :], moments[:, i, 0:1],
                                                       spread[:, 1, i:i + 1], ALU.subtract, ALU.mult)
                    last.then_inc(nodes_ready, 1)
                    dve.wait_ge(nodes_ready, c + 1)

                maxima_taken = [0]

                def take_max(l, m, layers_before=None):
                    ahead, c, t = m
                    k = following(l) if ahead else l
                    first_of_all = layers_before is None
                    if t == 0 and not first_of_all:
                        dve.wait_ge(largest_turned, step_number(k, c) - 1)
                    if t % PER == 0:
                        dve.wait_ge(al_scaled, CHUNKS * k.number + t // PER + 1)
                    if streamed:
                        number = maxima_taken[0] if first_of_all else len(BEFORE_LAYERS) + SLOTS * l.number + maxima_taken[0]
                        dve.wait_ge(max_tile_in, 16 * number + 16)
                    maxima_taken[0] += 1
                    code = max_tile[:, :] if streamed else counts[:, t, chunk_columns(c)]
                    own, al_s = largest[:, parity(k, c), :], al_tiny[:, k.second, t:t + 1]
                    done, count = maxed_at(l, m)
                    if t == 0:
                        ins = nc.vector.tensor_scalar(own, code, al_s, None, ALU.min)
                    else:
                        dve.wait_ge(done, count - 1)
                        ins = nc.vector.scalar_tensor_tensor(out=own, in0=code, scalar=al_s, in1=own, op0=ALU.min, op1=ALU.max)
                    ins.then_inc(done, 1)

                def columns(l, c):
                    g = step_number(l, c)
                    first = isinstance(g, int) and g == 0
                    dve.wait_ge(largest_turned, g + 1)
                    nc.vector.tensor_reduce(out=peak[:, 0:4], in_=psum[0:LANES, START, 0:4 * LANES].rearrange("p (i s) -> p i s", s=LANES),
                                            axis=AX, op=ALU.max).then_inc(col_step, 1)
                    nc.vector.tensor_reduce(out=peak[:, 4:5], in_=psum[0:LANES, START + 1, 0:LANES],
                                            axis=AX, op=ALU.max).then_inc(col_step, 1)
                    al_d = al[:, l.second, tile_range(c), 1]
                    if not first:
                        dve.wait_ge(rows_spread, 3 * g)
                    dve.wait_ge(col_step, 5 * g + 2)
                    nc.vector.tensor_scalar(row_cols[:, 0, :], peak[:, :], HUGE, None, ALU.mult).then_inc(col_step, 1)
                    dve.wait_ge(col_step, 5 * g + 3)
                    nc.vector.tensor_tensor(z_col[:, :], row_cols[:, 0, :], al_d, ALU.add).then_inc(col_step, 1)
                    dve.wait_ge(col_step, 5 * g + 4)
                    nc.vector.tensor_scalar(z_col[:, :], z_col[:, :], 0.0, (1 - SLOPE) / SLOPE, ALU.max, ALU.mult).then_inc(col_step, 1)
                    dve.wait_ge(col_step, 5 * g + 5)
                    nc.vector.tensor_tensor(z_col[:, :], z_col[:, :], row_cols[:, 0, :], ALU.add).then_inc(col_done, 1)
                    dve.wait_ge(col_done, g + 1)
                    nc.vector.tensor_scalar(row_cols[:, 1, :], z_col[:, :], SLOPE, None, ALU.mult).then_inc(cols_ready, 1)

                def exponent(l, c, t):
                    g = step_number(l, c)
                    if t == 0:
                        dve.wait_ge(rows_ready, g + 1)
                    dve.wait_ge(distance_ready, TILES * g + t + 1)
                    slot = ring[0:LANES, (TILES * c + t) % RING, :]
                    nc.vector.scalar_tensor_tensor(out=slot, in0=bent_row[:, parity(l, c), :], scalar=al_fifth[:, l.second, t:t + 1],
                                                   in1=slot, op0=ALU.subtract, op1=ALU.min).then_inc(exponent_ready, 1)

                def weigh(l, c, t):
                    g = step_number(l, c)
                    dve.wait_ge(exp_ready, TILES * g + t + 1)
                    slot = ring[0:LANES, (TILES * c + t) % RING, :]
                    if streamed:
                        dve.wait_ge(weigh_tile_in, 16 * (TILES * g + t) + 16)
                    code = weigh_tile[:, :] if streamed else counts[:, t, chunk_columns(c)]
                    nc.vector.scalar_tensor_tensor(out=slot, in0=code, scalar=1.0, in1=slot,
                                                   op0=ALU.add, op1=ALU.mult).then_inc(weight_ready, 1)

                def denominators(l, c):
                    g = step_number(l, c)
                    dve.wait_ge(tile_used, TILES * g + 2 * TILES)
                    dve.wait_ge(nodes_ready, g + CHUNKS)
                    for b, n in ((0, 3), (1, 2)):
                        last = nc.vector.tensor_scalar(
                            denom[:, 3 * b:3 * b + n],
                            psum[0:LANES, SUMS + 2 * parity(l, c) + b, 0:n * (FEAT + 1)].rearrange("p (i f) -> p i f", f=FEAT + 1)[:, :, FEAT],
                            2 * SOFTMAX_EPS, None, ALU.add)
                    last.then_inc(denom_step, 1)
                    dve.wait_ge(denom_step, g + 1)
                    nc.vector.reciprocal(denom[:, :], denom[:, :]).then_inc(denom_ready, 1)

                def add_x(c):
                    dve.wait_ge(sigmoid_ready, c + 1)
                    dve.wait_ge(x_again, 16 * c + 16)
                    nc.vector.tensor_tensor(result, result, x_chunk, ALU.add).then_inc(result_ready, 1)

                def layer(l):
                    last_layer = isinstance(l.number, int)
                    maxima_taken[0] = 0
                    exponent(l, 0, 0)
                    exponent(l, 0, 1)
                    for slot, these in enumerate(in_slots(last_layer)):
                        c, t = divmod(slot, TILES)
                        for m in these:
                            take_max(l, m, True)
                        weigh(l, c, t)
                        if slot + 2 < SLOTS:
                            exponent(l, *divmod(slot + 2, TILES))
                        if c and t == DENOMINATORS:
                            denominators(l, c - 1)
                        if c < CHUNKS - 1 and t == COLUMNS:
                            columns(l, c + 1)
                        if last_layer and c and t == ADD_X:
                            add_x(c - 1)
                    if last_layer:
                        denominators(l, CHUNKS - 1)
                        add_x(CHUNKS - 1)
                        return
                    for n, these in enumerate(AT_END):
                        for m in these:
                            take_max(l, m, True)
                        if n == 0:
                            denominators(l, CHUNKS - 1)
                        if n == 3:
                            columns(following(l), 0)

                normalise(0)
                for c in range(CHUNKS):
                    if c + 1 < CHUNKS:
                        normalise(c + 1)
                    for m in BEFORE_LAYERS:
                        if m[2] // PER == c:
                            take_max(FIRST, m)
                columns(FIRST, 0)
                with dve.Fori(0, LAYERS // 2) as pair:
                    for second in range(2):
                        layer(Layer(2 * pair + second, second, pair))
                layer(LAST)

        @block.tensor
        def _(pe):
            with taken(pe, whole, whole_ready, when):
                def turn_nodes(f, rows_read=None):
                    pe.wait_ge(nodes_ready, f + 1)
                    if rows_read is not None:
                        pe.wait_ge(rows_ready, rows_read)
                    for i in range(PER):
                        last = nc.tensor.transpose(piece(FINISH, i, 128), node_major[:, i, :], ident[0:LANES, 0:LANES])
                    last.then_inc(nodes_turned, 1)

                def dense(w, copied):
                    copied()
                    nc.tensor.matmul(psum[:, FINISH, 0:4 * LANES], w, feat_major[:, 0:4 * LANES], start=True, stop=True)
                    nc.tensor.matmul(psum[:, FINISH + 1, 0:LANES], w, feat_major[:, 4 * LANES:WIDE], start=True, stop=True).then_inc(dense_ready, 1)

                def make_hidden(f, k, first, frees_ring=False):
                    if first:
                        pe.wait_ge(weights_in, 32 * k + 32)
                    for i in range(PER):
                        at = (FEAT + 2) * (i % 3)
                        last = nc.tensor.matmul(psum[0:LANES, FINISH + i // 3, at:at + FEAT + 2], feat_major[:, LANES * i:LANES * (i + 1)],
                                                weights[:, :], start=True, stop=True)
                        if i == 0 and frees_ring:
                            last.then_inc(tile_used, TILES // CHUNKS)
                    last.then_inc(hidden_mm, 1)

                pe.wait_ge(consts_in, 64)
                for c in range(CHUNKS):
                    turn_nodes(c)
                    dense(enc_w[:, 0, :], lambda: pe.wait_ge(feats_ready, c + 1))
                    dense(enc_w[:, 1, :], lambda: pe.wait_ge(dense_copied, 3 * c + 1))
                    dense(enc_w[:, 2, :], lambda: pe.wait_ge(dense_copied, 3 * c + 2))
                    pe.wait_ge(dense_copied, 3 * c + 3)
                    make_hidden(c, 0, c == 0, frees_ring=True)
                    pe.wait_ge(hidden_ready, c + 1)

                def turn_largest(l, c):
                    g = step_number(l, c)
                    pe.wait_ge(*maxed_at(l, (0, c, TILES - 1)))
                    if not (isinstance(g, int) and g == 0):
                        pe.wait_ge(rows_ready, g)
                    if isinstance(l.number, int) and l.number == LAYERS - 1:
                        if c > 1:
                            pe.wait_ge(sigmoid_ready, c - 1)
                        pe.wait_ge(hidden_ready, CHUNKS * LAYERS)
                    else:
                        pe.wait_ge(hidden_ready, CHUNKS * (l.number + 1) + max(c - 1, 0))
                    for i in range(PER):
                        last = nc.tensor.transpose(piece(START, i), largest[:, parity(l, c), LANES * i:LANES * (i + 1)], ident[0:LANES, 0:LANES])
                    last.then_inc(largest_turned, 1)

                def spread_rows(l, c):
                    g = step_number(l, c)
                    pe.wait_ge(cols_ready, g + 1)
                    for q in range(2 * PER):
                        last = nc.tensor.transpose(piece(START, q), row_cols[:, q // PER, q % PER:q % PER + 1].broadcast_to([LANES, LANES]),
                                                   ident[0:LANES, 0:LANES])
                        if q % PER_BANK == PER_BANK - 1 or q == 2 * PER - 1:
                            last.then_inc(rows_spread, 1)

                def add_tile(l, c, t):
                    g = step_number(l, c)
                    pe.wait_ge(weight_ready, TILES * g + t + 1)
                    if t == 0:
                        pe.wait_ge(nodes_ready, g + CHUNKS - 1)
                    for i in range(PER):
                        last = nc.tensor.matmul(sums(parity(l, c), i), ring[0:LANES, (TILES * c + t) % RING, LANES * i:LANES * (i + 1)],
                                                hidden[0:LANES, l.second, t, :], start=t == 0 and i % 3 == 0, stop=t == TILES - 1,
                                                skip_group_check=True)
                    last.then_inc(tile_used, 1)

                def rows_used(l, c):
                    return step_number(l, min(c + 1, CHUNKS - 1)) + 1

                def finish_next(l, c):
                    f = step_number(following(l), c)
                    yield lambda: turn_nodes(f, rows_used(l, c))

                    def hid():
                        pe.wait_ge(feats_ready, f + 1)
                        make_hidden(f, l.number + 1, c == 0)
                    yield hid

                def finish_decoder(c):
                    f = LAYERS * CHUNKS + c
                    yield lambda: turn_nodes(f, rows_used(LAST, c))

                    def first():
                        pe.wait_ge(dec_in, 32)
                        dense(dec_w[:, 0, :], lambda: pe.wait_ge(feats_ready, f + 1))
                    yield first
                    yield lambda: dense(dec_w[:, 1, :], lambda: pe.wait_ge(dense_copied, 3 * CHUNKS + 2 * c + 1))

                    def logits():
                        pe.wait_ge(dense_copied, 3 * CHUNKS + 2 * c + 2)
                        pe.wait_ge(ones_set, 3)
                        for i in range(PER):
                            at = psum[0:LANES, FINISH + i // 4, FEAT * (i % 4):FEAT * (i % 4 + 1)]
                            nc.tensor.matmul(at, feat_major[:, LANES * i:LANES * (i + 1)], dec_w[:, 2, :], start=i % 4 == 0, stop=False,
                                             skip_group_check=True)
                            last = nc.tensor.matmul(at, one_row, dec_row, start=False, stop=True, skip_group_check=True)
                        last.then_inc(hidden_mm, 1)
                    yield logits

                def layer(l):
                    last_layer = isinstance(l.number, int)
                    finish = lambda c: list(finish_decoder(c) if last_layer else finish_next(l, c))
                    for slot in range(SLOTS):
                        c, t = divmod(slot, TILES)
                        if t == 0:
                            parts = finish(c - 1) if c else []
                        if parts and t in (DECODER_PE if last_layer else NEXT_PE):
                            parts.pop(0)()
                        if c < CHUNKS - 1 and t == TURN_MAX:
                            turn_largest(l, c + 1)
                        if c < CHUNKS - 1 and t == SPREAD:
                            spread_rows(l, c + 1)
                        add_tile(l, c, t)
                    for part in finish(CHUNKS - 1):
                        part()
                    if not last_layer:
                        turn_largest(following(l), 0)
                        spread_rows(following(l), 0)

                pe.wait_ge(ones_set, 2)
                turn_largest(FIRST, 0)
                spread_rows(FIRST, 0)
                with pe.Fori(0, LAYERS // 2) as pair:
                    for second in range(2):
                        layer(Layer(2 * pair + second, second, pair))
                layer(LAST)

        @block.scalar
        def _(act):
            with taken(act, whole, whole_ready, when):
                def copy_features(func, bias, copied):
                    nc.scalar.activation(feat_major[:, 0:4 * LANES], psum[:, FINISH, 0:4 * LANES], func, bias=bias)
                    yield
                    nc.scalar.activation(feat_major[:, 4 * LANES:WIDE], psum[:, FINISH + 1, 0:LANES], func, bias=bias).then_inc(copied, 1)
                    yield

                def copy_feats(f, bias):
                    act.wait_ge(nodes_turned, f + 1)
                    yield from copy_features(ACT.Relu, bias, feats_ready)

                def copy_dense(number, func, bias):
                    act.wait_ge(dense_ready, number + 1)
                    yield from copy_features(func, bias, dense_copied)

                def copy_hidden(k, c):
                    f = step_number(k, c)
                    al_k, tiny_k, minus_k, fifth_k = (a[:, k.second] for a in (al, al_tiny, al_minus, al_fifth))
                    hidden_k = hidden[0:LANES, k.second]
                    act.wait_ge(hidden_mm, f + 1)
                    for i, n in ((0, 3), (1, 2)):
                        tiles = slice(PER * c + 3 * i, PER * c + 3 * i + n)
                        nc.scalar.activation(al_k[:, tiles, :], fresh(i, FEAT, FEAT + 2), ACT.Copy).then_inc(al_ready, 1)
                    own = slice(PER * c, PER * (c + 1))
                    act.wait_ge(al_ready, 2 * f + 2)
                    nc.scalar.mul(tiny_k[:, own], al_k[:, own, 0], TINY)
                    nc.scalar.mul(minus_k[:, own], al_k[:, own, 0], -1.0)
                    nc.scalar.mul(fifth_k[:, own], al_k[:, own, 0], SLOPE).then_inc(al_scaled, 1)
                    yield
                    nc.scalar.activation(hidden_k[:, PER * c:PER * c + 3, 0:FEAT], fresh(0, 0, FEAT), ACT.Copy)
                    yield
                    nc.scalar.activation(hidden_k[:, PER * c + 3:PER * (c + 1), 0:FEAT], fresh(1, 0, FEAT), ACT.Copy).then_inc(hidden_ready, 1)
                    yield

                def run(parts):
                    for _ in parts:
                        pass

                act.wait_ge(consts_in, 64)
                for c in range(CHUNKS):
                    act.wait_ge(variance_ready, c + 1)
                    nc.scalar.activation(spread[:, 1, :], spread[:, 0, :], ACT.Sqrt).then_inc(root_ready, 1)
                    run(copy_feats(c, 0.0))
                    for k, func in enumerate((ACT.Relu, ACT.Relu, ACT.Identity)):
                        run(copy_dense(3 * c + k, func, enc_bias[:, k:k + 1]))
                    run(copy_hidden(FIRST, c))

                def copy_rows(l, c):
                    g = step_number(l, c)
                    if not (isinstance(g, int) and g == 0):
                        act.wait_ge(distance_ready, TILES * g)
                    bent = bent_row[:, parity(l, c), :]
                    act.wait_ge(rows_spread, 3 * g + 1)
                    nc.scalar.activation(top_row[:, 0:4 * LANES], psum[0:LANES, START, 0:4 * LANES], ACT.Copy)
                    act.wait_ge(rows_spread, 3 * g + 2)
                    nc.scalar.activation(top_row[:, 4 * LANES:WIDE], psum[0:LANES, START + 1, 0:LANES], ACT.Copy)
                    nc.scalar.activation(bent[:, 0:3 * LANES], psum[0:LANES, START + 1, LANES:4 * LANES], ACT.Copy)
                    act.wait_ge(rows_spread, 3 * g + 3)
                    last = nc.scalar.activation(bent[:, 3 * LANES:WIDE], psum[0:LANES, START + 2, 0:2 * LANES], ACT.Copy)
                    last.then_inc(rows_ready, 1)

                def distance(l, c, t):
                    slot = TILES * c + t
                    act.wait_ge(tile_used, TILES + SLOTS * l.number + max(slot - RING + 1, 0))
                    if t == 0:
                        act.wait_ge(rows_ready, step_number(l, c) + 1)
                    nc.scalar.activation(ring[0:LANES, (TILES * c + t) % RING, :], top_row[:, :], ACT.Identity,
                                         bias=al_minus[:, l.second, t:t + 1]).then_inc(distance_ready, 1)

                def clamp(l, c, t):
                    g = step_number(l, c)
                    act.wait_ge(exponent_ready, TILES * g + t + 1)
                    slot = ring[0:LANES, (TILES * c + t) % RING, :]
                    nc.scalar.activation(slot, slot, ACT.Relu).then_inc(clamped, 1)

                def exp(l, c, t):
                    g = step_number(l, c)
                    act.wait_ge(clamped, TILES * g + t + 1)
                    slot = ring[0:LANES, (TILES * c + t) % RING, :]
                    nc.scalar.activation(slot, slot, ACT.Exp, scale=-1.0).then_inc(exp_ready, 1)

                def divide(l, c):
                    g = step_number(l, c)
                    act.wait_ge(denom_ready, g + 1)
                    act.wait_ge(nodes_turned, g + CHUNKS)
                    for i in range(PER):
                        last = nc.scalar.activation(node_major[:, i, :], sums(parity(l, c), i, 0, FEAT), ACT.Copy, scale=denom[:, i:i + 1])
                        if i < PER - 1:
                            yield
                    last.then_inc(nodes_ready, 1)
                    yield

                def finish_next(l, c):
                    yield from divide(l, c)
                    yield from copy_feats(step_number(following(l), c), conv_bias[:, bass.ds(l.number, 1)])
                    yield from copy_hidden(following(l), c)

                def finish_decoder(c):
                    yield from divide(LAST, c)
                    yield from copy_feats(LAYERS * CHUNKS + c, conv_bias[:, LAYERS - 1:LAYERS])
                    for k in range(2):
                        yield from copy_dense(3 * CHUNKS + 2 * c + k, ACT.Relu, dec_bias[:, k:k + 1])
                    act.wait_ge(hidden_mm, LAYERS * CHUNKS + c + 1)
                    act.wait_ge(dec_in, 32)
                    if c:
                        act.wait_ge(stored, 16 * c)
                    nc.scalar.activation(result[:, 0:4 * FEAT], psum[0:LANES, FINISH, 0:4 * FEAT], ACT.Sigmoid)
                    yield
                    nc.scalar.activation(result[:, 4 * FEAT:5 * FEAT], psum[0:LANES, FINISH + 1, 0:FEAT], ACT.Sigmoid).then_inc(sigmoid_ready, 1)
                    yield

                def layer(l):
                    last_layer = isinstance(l.number, int)
                    finish = lambda c: finish_decoder(c) if last_layer else finish_next(l, c)
                    for slot in range(LEAD):
                        distance(l, *divmod(slot, TILES))
                    clamp(l, 0, 0)
                    for slot in range(SLOTS):
                        c, t = divmod(slot, TILES)
                        exp(l, c, t)
                        if slot + 1 < SLOTS:
                            clamp(l, *divmod(slot + 1, TILES))
                        if slot + LEAD < SLOTS:
                            distance(l, *divmod(slot + LEAD, TILES))
                        if c and t == 0:
                            parts = finish(c - 1)
                        if c:
                            for _ in range((DECODER_ACT if last_layer else NEXT_ACT).count(t)):
                                next(parts)
                        if c < CHUNKS - 1 and t == ROWS:
                            copy_rows(l, c + 1)
                    run(finish(CHUNKS - 1))
                    if not last_layer:
                        copy_rows(following(l), 0)

                copy_rows(FIRST, 0)
                with act.Fori(0, LAYERS // 2) as pair:
                    for second in range(2):
                        layer(Layer(2 * pair + second, second, pair))
                layer(LAST)


Layer = namedtuple("Layer", "number second pair")
FIRST, LAST = Layer(0, 0, 0), Layer(LAYERS - 1, 0, LAYERS // 2)


def following(l):
    return Layer(l.number + 1, 1 - l.second, l.pair + l.second)


def step_number(l, c):
    return CHUNKS * l.number + c


def parity(l, c):
    return (CHUNKS * l.second + c) % 2


def alike_before(l, c):
    return CHUNKS * l.pair + (CHUNKS * l.second + c) // 2


def tile_range(c):
    return slice(PER * c, PER * (c + 1))


def chunk_columns(c):
    return slice(WIDE * c, WIDE * (c + 1))


_INS = ["x", "src", "dst", "L0_gnn_enc_W", "L0_gnn_enc_b", "L0_gnn_conv_W", "L0_gnn_conv_att_src",
        "L0_gnn_conv_att_dst", "L0_gnn_conv_b", "L0_gnn_dec_W", "L0_gnn_dec_b"]


def kernel(**inputs):
    import numpy as _np
    import concourse.bacc as _bacc
    from concourse import mybir as _mybir
    from concourse.bass_utils import run_bass_kernel_spmd as _run

    nc = _bacc.Bacc("TRN2", target_bir_lowering=False, num_devices=1)
    arrays, args = {}, []
    for name in _INS:
        a = _np.ascontiguousarray(inputs[name])
        arrays[f"in_{name}"] = a
        args.append(nc.dram_tensor(f"in_{name}", a.shape, _mybir.dt.from_np(a.dtype), kind="ExternalInput").ap())
    args.append(nc.dram_tensor("out_0", (NODES, FEAT), F32, kind="ExternalOutput").ap())
    nc.disable_value_cache = True
    gat_program(nc, *args)
    r = _run(nc, [arrays], core_ids=[0])
    return r.results[0]["out_0"]
```

```python
import concourse.bass as bass
from concourse import mybir
from collections import namedtuple
from contextlib import ExitStack

F32 = mybir.dt.float32
I32 = mybir.dt.int32
U32 = mybir.dt.uint32
I16 = mybir.dt.int16
I8 = mybir.dt.int8
BF16 = mybir.dt.bfloat16
ALU = mybir.AluOpType
ACT = mybir.ActivationFunctionType
AX = mybir.AxisListType.X

NODES, FEAT, EDGES, LAYERS = 3125, 128, 53125, 9
SLOPE, LN_EPS, SOFTMAX_EPS = 0.2, 1e-5, 1e-16

LANES = 125
TILES = NODES // LANES
CHUNKS = 5
PER = TILES // CHUNKS
WIDE = PER * LANES


GRAIN = 25
ROWS = EDGES // GRAIN
ROWS_PER_LANE = ROWS // LANES
EDGES_PER_LANE = EDGES // LANES
BLOCK = 20
BLOCKS = -(-NODES // BLOCK)
TURN = 4
LAST_BASE = NODES - BLOCK
LAST_NEW = NODES - BLOCK * (BLOCKS - 1)
HALF = 80
WINDOW = 512
FETCHED = WINDOW - BLOCK
PASSES = WINDOW // 128
CODES = BLOCK * TILES
SHIFT = 12
NOWHERE = (1 << SHIFT) - 1

SLOTS = TILES * CHUNKS
RING = 10
LEAD = 6

MOST = 64

TINY = 2.0 ** -64
HUGE = 2.0 ** 64


def gat_program(nc, x, src, dst, enc_W, enc_b, conv_W, att_src, att_dst, conv_b, dec_W, dec_b, out):
    packed_d = nc.dram_tensor("packed_d", [EDGES + FETCHED], I32, kind="Internal").ap()
    firsts_d = nc.dram_tensor("firsts_d", [ROWS], F32, kind="Internal").ap()
    windows_d = nc.dram_tensor("windows_d", [ROWS, FETCHED], I32, kind="Internal").ap()
    counts_d = nc.dram_tensor("counts_d", [LANES, TILES, BLOCKS * BLOCK], F32, kind="Internal").ap()
    overlapping = bass.AP(tensor=packed_d.tensor, offset=0, ap=[[GRAIN, ROWS], [1, FETCHED]])

    top = ExitStack()
    with top:
        def sb(name, shape, dt=F32, stack=top):
            return stack.enter_context(nc.sbuf_tensor(name, shape, dt))

        def sem(name):
            return top.enter_context(nc.semaphore(name))

        ident = sb("ident", [128, 128])
        att_cols = sb("att_cols", [128, LAYERS, 2])
        whole = sb("whole", [1, 1], I32)
        whole_ready = sem("whole_ready")
        psum = top.enter_context(nc.psum_tensor("psum", [128, 8, 512], F32))

        resident = ExitStack()
        with resident:
            counts = sb("counts", [LANES, TILES, NODES], I8, resident)
            build_counts(nc, src, dst, conv_W, att_src, att_dst, packed_d, firsts_d, windows_d,
                         overlapping, counts, ident, att_cols, whole, whole_ready, psum, sem)
            network(nc, x, enc_W, enc_b, conv_W, conv_b, dec_W, dec_b, out, counts, None, ident, att_cols,
                    whole, whole_ready, psum, sem)

        build_counts_of_any(nc, src, dst, counts_d, whole, whole_ready, psum, lambda name: sem("any_" + name))
        network(nc, x, enc_W, enc_b, conv_W, conv_b, dec_W, dec_b, out, None, counts_d, ident, att_cols,
                whole, whole_ready, psum, lambda name: sem("any_" + name))


def run(parts):
    for _ in parts:
        pass


def taken(engine, whole, whole_ready, when):
    engine.wait_ge(whole_ready, 1)
    return engine.If(engine.value_load(whole[0:1, 0:1], min_val=0, max_val=1) == when)


def build_counts(nc, src, dst, conv_W, att_src, att_dst, packed_d, firsts_d, windows_d,
                 overlapping, counts, ident, att_cols, whole, whole_ready, psum, sem):
    scope = ExitStack()
    with scope:
        def sb(name, shape, dt=F32, stack=scope):
            return stack.enter_context(nc.sbuf_tensor(name, shape, dt))

        edges = sb("edges", [LANES, 2, EDGES_PER_LANE], I32)
        packed = sb("packed", [LANES, EDGES_PER_LANE], I32)
        firsts = sb("firsts", [LANES, ROWS_PER_LANE])
        all_firsts = sb("all_firsts", [HALF, ROWS])
        below = sb("below", [HALF, ROWS], BF16)
        base_i = sb("base_i", [HALF, 2], I32)
        base = sb("base", [HALF, 2])
        rows_below = sb("rows_below", [HALF, 2])
        own_code = sb("own_code", [HALF, 2])
        held = sb("held", [HALF, 2])
        ones = sb("window_ones", [HALF, 1])
        first_row = sb("first_row", [HALF, 2], U32)
        window = sb("window", [HALF, 2, WINDOW], I32)
        src_f = sb("src_f", [HALF, 2 * WINDOW])
        wrong = code_f = src_f
        tile_i = sb("tile_i", [HALF, 2 * WINDOW], I32)
        beyond = tile_i[0:1, 0:FETCHED]
        tile_f = sb("tile_f", [HALF, 2 * WINDOW])
        lane_f = sb("lane_f", [HALF, 2 * WINDOW])
        iota_i = sb("iota_i", [128, CODES], I16)
        lane_numbers = sb("lane_numbers", [128, LANES, PASSES], BF16)
        with ExitStack() as early:
            weights = sb("weights", [128, LAYERS, FEAT], stack=early)
            att = sb("att", [128, 2, LAYERS, FEAT], stack=early)
            product = sb("product", [128, FEAT], stack=early)
        lane_t = sb("lane_t", [128, 2 * HALF, PASSES], BF16)
        code_t = sb("code_t", [128, PASSES, 2 * HALF])
        lane_hot = sb("lane_hot", [128, 2, LANES, PASSES], BF16)
        code_hot = sb("code_hot", [128, 2, PASSES, CODES], BF16)

        edges_in = sem("edges_in")
        packed_out = sem("packed_out")
        windows_out = sem("windows_out")
        firsts_in = sem("firsts_in")
        weights_in = sem("weights_in")
        window_in = [sem("window_in0"), sem("window_in1")]
        pool_setup = sem("pool_setup")
        step = sem("dve_step")
        held_ready = sem("held_ready")
        held_summed = sem("held_summed")
        att_step = sem("att_step")
        packed_ready = sem("packed_ready")
        firsts_ready = sem("firsts_ready")
        first_row_ready = sem("first_row_ready")
        split_ready = sem("split_ready")
        turned = sem("turned")
        turned_copied = sem("turned_copied")
        hot_ready = sem("hot_ready")
        hot_used = sem("hot_used")
        block_stored = sem("block_stored")
        block = scope.enter_context(nc.Block())

        @block.sync
        def _(sp):
            sp.dma_start(edges[:, 1, :], dst.rearrange("(p j) -> p j", p=LANES)).then_inc(edges_in, 16)
            sp.dma_start(edges[:, 0, :], src.rearrange("(p j) -> p j", p=LANES)).then_inc(edges_in, 16)
            sp.dma_start(weights[:, :, :], conv_W.rearrange("l k n -> k l n")).then_inc(weights_in, 16)
            for k, a in enumerate((att_src, att_dst)):
                sp.dma_start(att[:, k, :, :].rearrange("p l n -> p (l n)"),
                             a.rearrange("(o l) n -> o (l n)", o=1).broadcast_to([128, LAYERS * FEAT])).then_inc(weights_in, 16)
            sp.wait_ge(firsts_ready, 1)
            sp.dma_start(firsts_d.rearrange("(p j) -> p j", p=LANES), firsts[:, :]).then_inc(firsts_in, 16)
            sp.wait_ge(packed_ready, 1)
            sp.wait_ge(pool_setup, 2)
            sp.dma_start(packed_d[0:EDGES].rearrange("(p j) -> p j", p=LANES), packed[:, :]).then_inc(packed_out, 16)
            sp.dma_start(packed_d[EDGES:EDGES + FETCHED].rearrange("(a j) -> a j", a=1), beyond).then_inc(packed_out, 16)
            sp.wait_ge(firsts_in, 16)
            sp.dma_start(all_firsts[:, :], firsts_d.rearrange("(a j) -> a j", a=1).broadcast_to([HALF, ROWS])).then_inc(firsts_in, 16)
            sp.wait_ge(packed_out, 32)
            sp.dma_start(windows_d[:, :], overlapping).then_inc(windows_out, 16)

        @block.gpsimd
        def _(pool):
            nc.gpsimd.iota(base_i[:, :], [[BLOCK * HALF, 2]], base=0, channel_multiplier=BLOCK).then_inc(pool_setup, 1)
            nc.gpsimd.memset(beyond, NOWHERE << SHIFT).then_inc(pool_setup, 1)
            nc.gpsimd.iota(iota_i[:, :], [[1, CODES]], base=0, channel_multiplier=0,
                           allow_small_or_imprecise_dtypes=True).then_inc(pool_setup, 1)
            nc.gpsimd.iota(lane_numbers[:, :, :], [[1, LANES], [0, PASSES]], base=0, channel_multiplier=0,
                           allow_small_or_imprecise_dtypes=True).then_inc(pool_setup, 1)
            nc.gpsimd.memset(ident[:, :], 0.0).then_inc(pool_setup, 1)
            pool.wait_ge(pool_setup, 5)
            nc.gpsimd.affine_select(out=ident[:, :], in_=ident[:, :], compare_op=ALU.not_equal, fill=1.0,
                                    base=0, pattern=[[-1, 128]], channel_multiplier=1).then_inc(pool_setup, 1)
            both = (1 << SHIFT) + 1
            for k in range(2):
                nc.gpsimd.iota(window[:, k, FETCHED:WINDOW], [[both, BLOCK]], base=BLOCK * HALF * k * both,
                               channel_multiplier=BLOCK * both).then_inc(pool_setup, 1)
            pool.wait_ge(first_row_ready, 1)
            pool.wait_ge(windows_out, 16)
            for k in range(2):
                nc.gpsimd.indirect_dma_start(
                    out=window[:, k, 0:FETCHED], out_offset=None, in_=windows_d[:, :],
                    in_offset=bass.IndirectOffsetOnAxis(ap=first_row[:, k:k + 1], axis=0)).then_inc(window_in[k], 16)
            for k in range(2):
                pool.wait_ge(window_in[k], 16)

        @block.vector
        def _(dve):
            done = [0]

            def link(ins):
                done[0] += 1
                ins.then_inc(step, 1)
                dve.wait_ge(step, done[0])

            dve.wait_ge(edges_in, 32)
            nc.vector.tensor_copy(firsts[:, :], edges[:, 1, :].rearrange("p (r g) -> p r g", g=GRAIN)[:, :, 0]).then_inc(firsts_ready, 1)
            nc.vector.scalar_tensor_tensor(out=packed[:, :], in0=edges[:, 1, :], scalar=float(1 << SHIFT), in1=edges[:, 0, :],
                                           op0=ALU.mult, op1=ALU.add).then_inc(packed_ready, 1)
            dve.wait_ge(pool_setup, 1)
            link(nc.vector.tensor_copy(base[:, :], base_i[:, :]))
            link(nc.vector.tensor_scalar(own_code[:, :], base[:, :], float(LAST_BASE), 0.0, ALU.subtract, ALU.max))
            link(nc.vector.tensor_scalar(own_code[:, :], own_code[:, :], float(TILES), None, ALU.mult))
            link(nc.vector.tensor_scalar(base[:, :], base[:, :], float(LAST_BASE), None, ALU.min))
            dve.wait_ge(firsts_in, 32)
            for k in range(2):
                link(nc.vector.tensor_scalar(below[:, :], all_firsts[:, :], base[:, k:k + 1], None, ALU.is_lt, ALU.add,
                                             accum_out=rows_below[:, k:k + 1]))
            nc.vector.tensor_scalar(first_row[:, :], rows_below[:, :], -1.0, 0.0, ALU.add, ALU.max).then_inc(first_row_ready, 1)

            dve.wait_ge(step, done[0])
            nc.vector.memset(product[:, :], 0.0).then_inc(att_step, 1)
            dve.wait_ge(att_step, 1)
            dve.wait_ge(weights_in, 48)
            for l in range(LAYERS):
                for k in range(2):
                    nc.vector.tensor_tensor_reduce(out=product[:, :], in0=weights[:, l, :], in1=att[:, k, l, :], scale=1.0, scalar=0.0,
                                                   op0=ALU.mult, op1=ALU.add,
                                                   accum_out=att_cols[:, l, k:k + 1]).then_inc(att_step, 1)
                    dve.wait_ge(att_step, 2 * l + k + 2)

            for k in range(2):
                dve.wait_ge(window_in[k], 16)
            dve.wait_ge(pool_setup, 8)
            flat = window[:, :, :].rearrange("p k w -> p (k w)")
            link(nc.vector.tensor_scalar(tile_i[:, :], flat, NOWHERE, None, ALU.bitwise_and))
            link(nc.vector.tensor_copy(src_f[:, :], tile_i[:, :]))
            link(nc.vector.tensor_scalar(tile_i[:, :], src_f[:, :], 0.5, 1.0 / LANES, ALU.add, ALU.mult))
            link(nc.vector.tensor_copy(tile_f[:, :], tile_i[:, :]))
            link(nc.vector.scalar_tensor_tensor(out=lane_f[:, :], in0=tile_f[:, :], scalar=-float(LANES), in1=src_f[:, :], op0=ALU.mult, op1=ALU.add))
            link(nc.vector.tensor_scalar(wrong[:, :], lane_f[:, :], 0.0, None, ALU.is_lt))
            link(nc.vector.tensor_tensor(tile_f[:, :], tile_f[:, :], wrong[:, :], ALU.subtract))
            nc.vector.scalar_tensor_tensor(out=lane_f[:, :], in0=wrong[:, :], scalar=float(LANES), in1=lane_f[:, :], op0=ALU.mult, op1=ALU.add).then_inc(split_ready, 1)
            dve.wait_ge(split_ready, 1)
            link(nc.vector.tensor_scalar(tile_i[:, :], flat, SHIFT, None, ALU.logical_shift_right))
            for k in range(2):
                half = slice(WINDOW * k, WINDOW * (k + 1))
                link(nc.vector.tensor_scalar(code_f[:, half], tile_i[:, half], base[:, k:k + 1], float(TILES), ALU.subtract, ALU.mult))
            nc.vector.tensor_tensor(code_f[:, :], code_f[:, :], tile_f[:, :], ALU.add).then_inc(split_ready, 1)

            dve.wait_ge(split_ready, 2)
            link(nc.vector.memset(ones[:, :], 1.0))
            for k in range(2):
                half = slice(WINDOW * k, WINDOW * (k + 1))
                link(nc.vector.tensor_scalar(tile_f[:, half], code_f[:, half], own_code[:, k:k + 1], None, ALU.is_ge))
                link(nc.vector.scalar_tensor_tensor(out=tile_f[:, half], in0=code_f[:, half], scalar=float(CODES), in1=tile_f[:, half],
                                                    op0=ALU.is_lt, op1=ALU.mult))
            dst_at = tile_i[:, :].rearrange("p (k w) -> p k w", k=2)
            in_block = tile_f[:, :].rearrange("p (k w) -> p k w", k=2)
            later = lane_f[:, :].rearrange("p (k w) -> p k w", k=2)
            dve.wait_ge(turned, 1)
            link(nc.vector.tensor_tensor(later[:, :, 0:FETCHED - MOST + 1], dst_at[:, :, MOST - 1:FETCHED], dst_at[:, :, 0:FETCHED - MOST + 1], ALU.is_gt))
            link(nc.vector.tensor_tensor(in_block[:, :, 0:FETCHED - MOST + 1], in_block[:, :, 0:FETCHED - MOST + 1], later[:, :, 0:FETCHED - MOST + 1], ALU.mult))
            link(nc.vector.tensor_tensor(later[:, :, 0:FETCHED - 1], dst_at[:, :, 1:FETCHED], dst_at[:, :, 0:FETCHED - 1], ALU.is_lt))
            link(nc.vector.tensor_tensor(in_block[:, :, 0:FETCHED - 1], in_block[:, :, 0:FETCHED - 1], later[:, :, 0:FETCHED - 1], ALU.subtract))
            nc.vector.tensor_reduce(out=held[:, :], in_=in_block, axis=AX, op=ALU.add).then_inc(held_ready, 1)
            dve.wait_ge(held_summed, 1)
            link(nc.vector.tensor_reduce(out=held[0:1, 0:1], in_=psum[0:1, 6, 0:2], axis=AX, op=ALU.add))
            nc.vector.tensor_scalar(whole[:, :], held[0:1, 0:1], float(EDGES + NODES), None, ALU.is_equal).then_inc(whole_ready, 1)

            dve.wait_ge(turned_copied, 2)

            def one_hots(b, odd):
                if not isinstance(b, int) or b > 1:
                    dve.wait_ge(hot_used, PASSES * b - PASSES)
                at = slice(b, b + 1) if isinstance(b, int) else bass.ds(b, 1)
                nc.vector.tensor_tensor(lane_hot[:, odd, :, :], lane_numbers[:, :, :], lane_t[:, at, :].broadcast_to([128, LANES, PASSES]),
                                        ALU.is_equal).then_inc(hot_ready, 1)
                for j in range(PASSES):
                    nc.vector.tensor_scalar(code_hot[:, odd, j, :], iota_i[:, :], code_t[:, j, at], None, ALU.is_equal).then_inc(hot_ready, 1)

            for b in range(TURN):
                one_hots(b, b % 2)
            with dve.Fori(1, BLOCKS // TURN) as turn:
                for b in range(TURN):
                    one_hots(TURN * turn + b, b % 2)
            for b in range(BLOCKS // TURN * TURN, BLOCKS):
                one_hots(b, b % 2)

        @block.tensor
        def _(pe):
            pe.wait_ge(pool_setup, 6)
            for n, part in enumerate((lane_f, code_f)):
                pe.wait_ge(split_ready, n + 1)
                for j in range(PASSES):
                    for k in range(2):
                        at = WINDOW * k + 128 * j
                        last = nc.tensor.transpose(psum[:, 2 * n + j // 2, 256 * (j % 2) + HALF * k:256 * (j % 2) + HALF * (k + 1)],
                                                   part[:, at:at + 128], ident[0:HALF, 0:HALF])
                last.then_inc(turned, 1)
            pe.wait_ge(held_ready, 1)
            nc.tensor.matmul(psum[0:1, 6, 0:2], ones[:, :], held[:, :], start=True, stop=True).then_inc(held_summed, 1)

            def count(b, odd):
                for j in range(PASSES):
                    pe.wait_ge(hot_ready, (PASSES + 1) * b + j + 2)
                    last = nc.tensor.matmul(psum[0:LANES, 4 + odd, 0:CODES], lane_hot[:, odd, :, j], code_hot[:, odd, j, :],
                                            start=j == 0, stop=j == PASSES - 1)
                    last.then_inc(hot_used, 1)

            count(0, 0)
            count(1, 1)
            with pe.Fori(1, (BLOCKS - 1) // 2) as pair:
                for odd in range(2):
                    pe.wait_ge(block_stored, 2 * pair - 1 + odd)
                    count(2 * pair + odd, odd)
            pe.wait_ge(block_stored, BLOCKS - 2)
            count(BLOCKS - 1, 0)

        @block.scalar
        def _(act):
            for n, part in enumerate((lane_t, code_t)):
                act.wait_ge(turned, n + 1)
                columns_first = part[:, :, :].rearrange("p c j -> p j c") if part is lane_t else part[:, :, :]
                nc.scalar.activation(columns_first.rearrange("p (a b) c -> p a b c", a=2),
                                     psum[:, 2 * n:2 * n + 2, :].rearrange("p a (b c) -> p a b c", b=2)[:, :, :, 0:2 * HALF],
                                     ACT.Copy).then_inc(turned_copied, 1)

            def store(bank, at, first_dst, dsts, number):
                act.wait_ge(hot_used, number * PASSES)
                nc.scalar.activation(counts[:, :, at].rearrange("p t i -> p i t"),
                                     psum[0:LANES, bank, first_dst * TILES:(first_dst + dsts) * TILES].rearrange("p (i t) -> p i t", t=TILES),
                                     ACT.Copy, scale=2.0, bias=-1.0).then_inc(block_stored, 1)

            with act.Fori(0, (BLOCKS - 1) // 2) as pair:
                for odd in range(2):
                    store(4 + odd, bass.ds(2 * BLOCK * pair + BLOCK * odd, BLOCK), 0, BLOCK, 2 * pair + odd + 1)
            store(4, slice(NODES - LAST_NEW, NODES), BLOCK - LAST_NEW, LAST_NEW, BLOCKS)


def build_counts_of_any(nc, src, dst, counts_d, whole, whole_ready, psum, sem):
    scope = ExitStack()
    with scope:
        def sb(name, shape, dt=F32):
            return scope.enter_context(nc.sbuf_tensor("any_" + name, shape, dt))

        COLUMNS = EDGES_PER_LANE + TILES
        src_i = sb("src_i", [LANES, COLUMNS], I32)
        dst_i = sb("dst_i", [LANES, COLUMNS], I32)
        tile_i = sb("tile_i", [LANES, COLUMNS], I32)
        src_f = sb("src_f", [LANES, COLUMNS])
        wrong = src_f
        tile_f = sb("tile_f", [LANES, COLUMNS])
        lane_f = sb("lane_f", [LANES, COLUMNS])
        code_f = sb("code_f", [LANES, COLUMNS])
        iota_i = sb("iota_i", [LANES, CODES], I16)
        lane_hot = sb("lane_hot", [LANES, LANES], BF16)
        code_hot = sb("code_hot", [LANES, CODES], BF16)
        block_counts = sb("block_counts", [LANES, TILES, BLOCK])

        edges_in = sem("edges_in")
        loops_set = sem("loops_set")
        step = sem("dve_step")
        hot_ready = sem("hot_ready")
        hot_used = sem("hot_used")
        block_copied = sem("block_copied")
        block_stored = sem("block_stored")
        block = scope.enter_context(nc.Block())

        @block.sync
        def _(sp):
            with taken(sp, whole, whole_ready, 0):
                sp.dma_start(dst_i[:, 0:EDGES_PER_LANE], dst.rearrange("(p j) -> p j", p=LANES)).then_inc(edges_in, 16)
                sp.dma_start(src_i[:, 0:EDGES_PER_LANE], src.rearrange("(p j) -> p j", p=LANES)).then_inc(edges_in, 16)
                with sp.Fori(0, BLOCKS) as b:
                    sp.wait_ge(block_copied, b + 1)
                    sp.dma_start(counts_d[:, :, bass.ds(BLOCK * b, BLOCK)], block_counts[:, :, :]).then_inc(block_stored, 16)
                sp.wait_ge(block_stored, 16 * BLOCKS)

        @block.gpsimd
        def _(pool):
            with taken(pool, whole, whole_ready, 0):
                for ends in (src_i, dst_i):
                    nc.gpsimd.iota(ends[:, EDGES_PER_LANE:COLUMNS], [[LANES, TILES]], base=0, channel_multiplier=1).then_inc(loops_set, 1)
                nc.gpsimd.iota(iota_i[:, :], [[1, CODES]], base=0, channel_multiplier=0,
                               allow_small_or_imprecise_dtypes=True).then_inc(loops_set, 1)

        @block.vector
        def _(dve):
            with taken(dve, whole, whole_ready, 0):
                done = [0]

                def link(ins):
                    done[0] += 1
                    ins.then_inc(step, 1)
                    dve.wait_ge(step, done[0])

                dve.wait_ge(edges_in, 32)
                dve.wait_ge(loops_set, 3)
                link(nc.vector.tensor_copy(src_f[:, :], src_i[:, :]))
                link(nc.vector.tensor_copy(code_f[:, :], dst_i[:, :]))
                link(nc.vector.tensor_scalar(tile_i[:, :], src_f[:, :], 0.5, 1.0 / LANES, ALU.add, ALU.mult))
                link(nc.vector.tensor_copy(tile_f[:, :], tile_i[:, :]))
                link(nc.vector.scalar_tensor_tensor(out=lane_f[:, :], in0=tile_f[:, :], scalar=-float(LANES), in1=src_f[:, :], op0=ALU.mult, op1=ALU.add))
                link(nc.vector.tensor_scalar(wrong[:, :], lane_f[:, :], 0.0, None, ALU.is_lt))
                link(nc.vector.tensor_tensor(tile_f[:, :], tile_f[:, :], wrong[:, :], ALU.subtract))
                link(nc.vector.scalar_tensor_tensor(out=lane_f[:, :], in0=wrong[:, :], scalar=float(LANES), in1=lane_f[:, :], op0=ALU.mult, op1=ALU.add))
                link(nc.vector.scalar_tensor_tensor(out=code_f[:, :], in0=code_f[:, :], scalar=float(TILES), in1=tile_f[:, :], op0=ALU.mult, op1=ALU.add))

                def one_hots(j):
                    at = slice(j, j + 1) if isinstance(j, int) else bass.ds(j, 1)
                    nc.vector.tensor_scalar(lane_hot[:, :], iota_i[:, 0:LANES], lane_f[:, at], None, ALU.is_equal).then_inc(hot_ready, 1)
                    nc.vector.tensor_scalar(code_hot[:, :], iota_i[:, :], code_f[:, at], None, ALU.is_equal).then_inc(hot_ready, 1)

                def one_block(b):
                    if not isinstance(b, int):
                        dve.wait_ge(hot_used, COLUMNS * b)
                        nc.vector.tensor_scalar(code_f[:, :], code_f[:, :], float(CODES), None, ALU.subtract).then_inc(step, 1)
                        dve.wait_ge(step, b + done[0])
                    one_hots(0)
                    with dve.Fori(1, COLUMNS) as j:
                        dve.wait_ge(hot_used, COLUMNS * b + j)
                        one_hots(j)

                one_block(0)
                with dve.Fori(1, BLOCKS) as b:
                    one_block(b)

        @block.tensor
        def _(pe):
            def add_column(b, j):
                pe.wait_ge(hot_ready, 2 * (COLUMNS * b + j) + 2)
                fixed = isinstance(j, int)
                nc.tensor.matmul(psum[0:LANES, 4, 0:CODES], lane_hot[:, :], code_hot[:, :], start=fixed and j == 0,
                                 stop=fixed and j > 0, skip_group_check=True).then_inc(hot_used, 1)

            def one_block(b):
                if not isinstance(b, int):
                    pe.wait_ge(block_copied, b)
                add_column(b, 0)
                with pe.Fori(1, COLUMNS - 1) as j:
                    add_column(b, j)
                add_column(b, COLUMNS - 1)

            with taken(pe, whole, whole_ready, 0):
                one_block(0)
                with pe.Fori(1, BLOCKS) as b:
                    one_block(b)

        @block.scalar
        def _(act):
            def one_block(b):
                act.wait_ge(hot_used, COLUMNS * b + COLUMNS)
                if not isinstance(b, int):
                    act.wait_ge(block_stored, 16 * b)
                nc.scalar.activation(block_counts[:, :, :].rearrange("p t i -> p i t"),
                                     psum[0:LANES, 4, 0:CODES].rearrange("p (i t) -> p i t", t=TILES),
                                     ACT.Copy, scale=2.0, bias=-1.0).then_inc(block_copied, 1)

            with taken(act, whole, whole_ready, 0):
                one_block(0)
                with act.Fori(1, BLOCKS) as b:
                    one_block(b)


def network(nc, x, enc_W, enc_b, conv_W, conv_b, dec_W, dec_b, out, counts, counts_d, ident, att_cols,
            whole, whole_ready, psum, sem):
    scope = ExitStack()
    with scope:
        streamed = counts is None
        when = 0 if streamed else 1

        def sb(name, shape, dt=F32):
            return scope.enter_context(nc.sbuf_tensor("any_" + name if streamed else name, shape, dt))

        hidden = sb("hidden", [128, 2, TILES, FEAT + 1])
        al = sb("al", [LANES, 2, TILES, 2])
        al_tiny = sb("al_tiny", [LANES, 2, TILES])
        al_minus = sb("al_minus", [LANES, 2, TILES])
        al_fifth = sb("al_fifth", [LANES, 2, TILES])
        ring = sb("ring", [128, RING, WIDE])
        top_row = sb("top_row", [LANES, WIDE])
        bent_row = sb("bent_row", [LANES, 2, WIDE])
        largest = sb("largest", [LANES, 2, WIDE])
        node_major = sb("node_major", [LANES, PER, FEAT])
        feat_major = sb("feat_major", [128, WIDE])
        weights = sb("layer_weights", [128, FEAT + 2])
        peak = sb("peak", [LANES, PER])
        z_col = sb("z_col", [LANES, PER])
        row_cols = sb("row_cols", [LANES, 2, PER])
        denom = sb("denom", [LANES, PER])
        conv_bias = sb("conv_bias", [128, LAYERS])
        enc_bias = sb("enc_bias", [128, 3])
        dec_bias = sb("dec_bias", [128, 3])

        enc_w = ring[:, 0, 0:3 * FEAT].rearrange("p (k n) -> p k n", k=3)
        feats = [feat_major[:, :], ring[:, 1, :]]
        nodes = [node_major[:, :, :], bent_row[:, :, :].rearrange("p a w -> p (a w)")[:, 0:PER * FEAT].rearrange("p (i f) -> p i f", f=FEAT)]
        stats = ring[0:LANES, 3, 0:6 * TILES].rearrange("p (t k) -> p t k", k=6)
        moments = ring[0:LANES, 3, 6 * TILES:8 * TILES].rearrange("p (t k) -> p t k", k=2)
        spread = ring[0:LANES, 3, 8 * TILES:11 * TILES].rearrange("p (k t) -> p k t", k=3)
        x_all = hidden[0:LANES, 1, :, 0:FEAT]
        spare = hidden[:, LAYERS % 2, :, :].rearrange("p t f -> p (t f)")
        dec_w = spare[:, 0:3 * FEAT].rearrange("p (k n) -> p k n", k=3)
        x_chunk = spare[0:LANES, 384:384 + PER * FEAT]
        result = spare[0:LANES, 1024:1024 + PER * FEAT]
        dec_row = spare[0:1, 1664:1664 + FEAT]
        one_row = spare[0:1, 1800:1800 + LANES]

        if streamed:
            max_tile = sb("max_tile", [LANES, WIDE])
            weigh_tile = sb("weigh_tile", [LANES, WIDE])
            max_tile_in = sem("max_tile_in")
            weigh_tile_in = sem("weigh_tile_in")

        consts_in = sem("consts_in")
        x_in = [sem(f"x_in{c}") for c in range(CHUNKS)]
        weights_in = sem("layer_weights_in")
        dec_in = sem("dec_in")
        x_again = sem("x_again")
        stored = sem("stored")
        ones_set = sem("ones_set")
        ln_step = sem("ln_step")
        variance_ready = sem("variance_ready")
        root_ready = sem("root_ready")
        nodes_ready = sem("nodes_ready")
        nodes_turned = sem("nodes_turned")
        feats_ready = sem("feats_ready")
        dense_ready = sem("dense_ready")
        dense_copied = sem("dense_copied")
        hidden_mm = sem("hidden_mm")
        hidden_ready = sem("hidden_ready")
        al_ready = sem("al_ready")
        al_scaled = sem("al_scaled")
        maxed = [sem("maxed_even"), sem("maxed_odd")]
        largest_turned = sem("largest_turned")
        col_step = sem("col_step")
        col_done = sem("col_done")
        cols_ready = sem("cols_ready")
        rows_spread = sem("rows_spread")
        rows_ready = sem("rows_ready")
        distance_ready = sem("distance_ready")
        exponent_ready = sem("exponent_ready")
        clamped = sem("clamped")
        exp_ready = sem("exp_ready")
        weight_ready = sem("weight_ready")
        tile_used = sem("tile_used")
        denom_step = sem("denom_step")
        denom_ready = sem("denom_ready")
        sigmoid_ready = sem("sigmoid_ready")
        result_ready = sem("result_ready")
        block = scope.enter_context(nc.Block())

        SUMS, FINISH, START = 0, 4, 5
        PER_BANK = 512 // LANES

        def piece(bank, i, n=LANES):
            return psum[0:n, bank + i // PER_BANK, LANES * (i % PER_BANK):LANES * (i % PER_BANK) + LANES]

        def sums(even_odd, i, a=0, b=FEAT + 1):
            at = (FEAT + 1) * (i % 3)
            return psum[0:LANES, SUMS + 2 * even_odd + i // 3, at + a:at + b]

        def fresh(second, i, a, b):
            n = 3 - i
            return psum[0:LANES, FINISH + 2 * second + i, 0:n * (FEAT + 2)].rearrange("p (t f) -> p t f", f=FEAT + 2)[:, :, a:b]

        EARLY = TILES - PER
        EXPONENTS_AHEAD = 4

        PAIRS = [range(slot, min(slot + 2, SLOTS)) for slot in range(0, SLOTS, 2)]

        def maxima(ahead, c, first=0, end=TILES):
            return [(ahead, c, t) for t in range(first, end)]

        def in_slots(last_layer):
            own = maxima(0, 1, EARLY) + maxima(0, 2) + maxima(0, 3) + maxima(0, 4)
            done = TILES * (CHUNKS - 1) - 13
            slots = [[] for _ in range(SLOTS)]
            for k, m in enumerate(own):
                slots[k * done // len(own)].append(m)
            if not last_layer:
                for k, m in enumerate(maxima(1, 0, 0, EARLY)):
                    slots[done + 4 + k * (SLOTS - 5 - done) // EARLY].append(m)
            return slots

        AT_END = [maxima(1, 1, 0, 4), maxima(1, 1, 4, 12), maxima(1, 0, EARLY), maxima(1, 1, 12, 14), maxima(1, 1, 14, EARLY)]
        BEFORE_LAYERS = [(0, to, t) for t in range(TILES) for to in (0, 1) if to == 0 or t < EARLY]

        DENOMINATORS, ADD_X = 0, 12
        NEXT_PE, NEXT_ACT = (6, 9, 9, 10, 10, 11), (3, 3, 4, 4, 5, 7, 8, 12, 12, 13)
        DECODER_PE, DECODER_ACT = (3, 5, 7, 9), (1, 1, 1, 1, 2, 4, 4, 6, 6, 8, 8, 10, 10)
        TURN_MAX, COLUMNS, SPREAD = 14, 15, (16, 17, 17)
        ENCODER = sorted(((c, stage) for c in range(CHUNKS) for stage in range(5)), key=lambda cs: (2 * cs[0] + cs[1], cs[0]))

        def dense_number(c, stage):
            return [cs for cs in ENCODER if 1 <= cs[1] <= 3].index((c, stage))

        def maxed_at(l, m):
            ahead, c, t = m
            k = following(l) if ahead else l
            return maxed[parity(k, c)], TILES * alike_before(k, c) + t + 1

        node_rows = lambda c: slice(c * WIDE, (c + 1) * WIDE)

        @block.sync
        def _(sp):
            with taken(sp, whole, whole_ready, when):
                for c in range(CHUNKS):
                    sp.dma_start(x_all[:, PER * c:PER * (c + 1), :],
                                 x[node_rows(c), :].rearrange("(t p) f -> p t f", p=LANES)).then_inc(x_in[c], 16)
                sp.dma_start(enc_w, enc_W.rearrange("k i n -> i k n")).then_inc(consts_in, 16)
                sp.dma_start(enc_bias[:, :], enc_b.rearrange("k f -> f k"), allow_slow_non_contiguous=True).then_inc(consts_in, 16)
                sp.dma_start(dec_bias[:, :], dec_b.rearrange("k f -> f k"), allow_slow_non_contiguous=True).then_inc(consts_in, 16)
                sp.dma_start(conv_bias[:, :], conv_b.rearrange("k f -> f k"), allow_slow_non_contiguous=True).then_inc(consts_in, 16)

                def load_tile(tile, loaded, used, count, c, t):
                    sp.wait_ge(used, count)
                    sp.dma_start(tile[:, :], counts_d[:, t, chunk_columns(c)]).then_inc(loaded, 16)

                def load_maxima(l, these, before):
                    for m in these:
                        used, count = maxed_at(l, before) if before else (ones_set, 1)
                        load_tile(max_tile, max_tile_in, used, count, m[1], m[2])
                        before = m
                    return before

                def stream_layer(l):
                    last_layer = isinstance(l.number, int)
                    before = (0, 1, EARLY - 1)
                    sp.wait_ge(*maxed_at(l, (0, 0, TILES - 1)))
                    slots = in_slots(last_layer)
                    for pair in PAIRS:
                        for slot in pair:
                            before = load_maxima(l, slots[slot], before)
                        for slot in pair:
                            load_tile(weigh_tile, weigh_tile_in, tile_used, TILES + SLOTS * l.number + slot, *divmod(slot, TILES))
                            if last_layer and slot % TILES == TILES - 1:
                                c = slot // TILES
                                if c:
                                    store_result(c - 1)
                                load_x(c)
                    if not last_layer:
                        load_maxima(l, sum(AT_END, []), before)

                def load_weights(k):
                    at = slice(k, k + 1) if isinstance(k, int) else bass.ds(k, 1)
                    sp.dma_start(weights[:, 0:FEAT], conv_W[at, :, :].rearrange("l k n -> (l k) n")).then_inc(weights_in, 16)
                    sp.dma_start(weights[:, FEAT:FEAT + 2], att_cols[:, at, :].rearrange("p l a -> p (l a)")).then_inc(weights_in, 16)

                def load_x(c):
                    sp.dma_start(x_chunk.rearrange("p (t f) -> p t f", f=FEAT),
                                 x[node_rows(c), :].rearrange("(t p) f -> p t f", p=LANES)).then_inc(x_again, 16)

                def store_result(c):
                    sp.wait_ge(result_ready, c + 1)
                    sp.dma_start(out[node_rows(c), :].rearrange("(t p) f -> p t f", p=LANES),
                                 result.rearrange("p (t f) -> p t f", f=FEAT)).then_inc(stored, 16)

                load_weights(0)
                if streamed:
                    load_maxima(FIRST, BEFORE_LAYERS, None)
                with sp.Fori(0, LAYERS // 2) as pair:
                    for second in range(2):
                        l = Layer(2 * pair + second, second, pair)
                        sp.wait_ge(hidden_mm, CHUNKS * l.number + CHUNKS)
                        load_weights(l.number + 1)
                        if streamed:
                            stream_layer(l)
                sp.wait_ge(tile_used, SLOTS * (LAYERS - 1) + TILES)
                sp.wait_ge(hidden_ready, CHUNKS * LAYERS)
                sp.dma_start(dec_w, dec_W.rearrange("k i n -> i k n")).then_inc(dec_in, 16)
                sp.dma_start(dec_row, dec_b[2:3, :]).then_inc(dec_in, 16)
                if streamed:
                    stream_layer(LAST)
                else:
                    load_x(0)
                    for c in range(1, CHUNKS):
                        store_result(c - 1)
                        load_x(c)
                store_result(CHUNKS - 1)
                sp.wait_ge(stored, 16 * CHUNKS)

        @block.gpsimd
        def _(pool):
            with taken(pool, whole, whole_ready, when):
                nc.gpsimd.memset(hidden[:, 0, :, FEAT:FEAT + 1], 1.0).then_inc(ones_set, 1)
                nc.gpsimd.memset(hidden[:, 1, :, FEAT:FEAT + 1], 1.0).then_inc(ones_set, 1)
                pool.wait_ge(tile_used, SLOTS * (LAYERS - 1) + TILES)
                nc.gpsimd.memset(one_row, 1.0).then_inc(ones_set, 1)

        @block.vector
        def _(dve):
            with taken(dve, whole, whole_ready, when):
                ln = [0]

                def link(ins):
                    ln[0] += 1
                    ins.then_inc(ln_step, 1)
                    dve.wait_ge(ln_step, ln[0])

                for c in range(CHUNKS):
                    dve.wait_ge(x_in[c], 16)
                    for t in range(PER * c, PER * (c + 1)):
                        last = nc.vector.bn_stats(stats[:, t, :], x_all[:, t, :])
                link(last)
                for t in range(TILES):
                    last = nc.vector.bn_aggr(moments[:, t, :], stats[:, t, :])
                link(last)
                nc.vector.tensor_scalar(spread[:, 0, :], moments[:, :, 1], LN_EPS, None, ALU.add).then_inc(variance_ready, 1)
                dve.wait_ge(root_ready, 1)
                link(nc.vector.reciprocal(spread[:, 2, :], spread[:, 1, :]))
                link(nc.vector.tensor_tensor(spread[:, 2, :], spread[:, 2, :], spread[:, 0, :], ALU.mult))
                link(nc.vector.tensor_tensor(spread[:, 2, :], spread[:, 2, :], spread[:, 1, :], ALU.add))
                link(nc.vector.tensor_scalar(spread[:, 2, :], spread[:, 2, :], 0.5, None, ALU.mult))
                link(nc.vector.reciprocal(spread[:, 1, :], spread[:, 2, :]))

                def normalise(c):
                    if c > 1:
                        dve.wait_ge(nodes_turned, c - 1)
                    for i in range(PER):
                        t = PER * c + i
                        last = nc.vector.tensor_scalar(nodes[c % 2][:, i, :], x_all[:, t, :], moments[:, t, 0:1],
                                                       spread[:, 1, t:t + 1], ALU.subtract, ALU.mult)
                    last.then_inc(nodes_ready, 1)

                maxima_taken = [0]

                def take_max(l, m, before_layers=False):
                    ahead, c, t = m
                    k = following(l) if ahead else l
                    if t == 0 and not before_layers:
                        dve.wait_ge(largest_turned, step_number(k, c) - 1)
                    if t % PER == 0:
                        dve.wait_ge(al_scaled, CHUNKS * k.number + t // PER + 1)
                    if streamed:
                        number = maxima_taken[0] if before_layers else len(BEFORE_LAYERS) + SLOTS * l.number + maxima_taken[0]
                        dve.wait_ge(max_tile_in, 16 * number + 16)
                    maxima_taken[0] += 1
                    code = max_tile[:, :] if streamed else counts[:, t, chunk_columns(c)]
                    own, al_s = largest[:, parity(k, c), :], al_tiny[:, k.second, t:t + 1]
                    done, count = maxed_at(l, m)
                    if t == 0:
                        ins = nc.vector.tensor_scalar(own, code, al_s, None, ALU.min)
                    else:
                        dve.wait_ge(done, count - 1)
                        ins = nc.vector.scalar_tensor_tensor(out=own, in0=code, scalar=al_s, in1=own, op0=ALU.min, op1=ALU.max)
                    ins.then_inc(done, 1)

                def columns(l, c):
                    g = step_number(l, c)
                    first = isinstance(g, int) and g == 0
                    dve.wait_ge(largest_turned, g + 1)
                    nc.vector.tensor_reduce(out=peak[:, 0:4], in_=psum[0:LANES, START, 0:4 * LANES].rearrange("p (i s) -> p i s", s=LANES),
                                            axis=AX, op=ALU.max).then_inc(col_step, 1)
                    nc.vector.tensor_reduce(out=peak[:, 4:5], in_=psum[0:LANES, START + 1, 0:LANES],
                                            axis=AX, op=ALU.max).then_inc(col_step, 1)
                    al_d = al[:, l.second, tile_range(c), 1]
                    if not first:
                        dve.wait_ge(rows_spread, 3 * g)
                    dve.wait_ge(col_step, 5 * g + 2)
                    nc.vector.tensor_scalar(row_cols[:, 0, :], peak[:, :], HUGE, None, ALU.mult).then_inc(col_step, 1)
                    dve.wait_ge(col_step, 5 * g + 3)
                    nc.vector.tensor_tensor(z_col[:, :], row_cols[:, 0, :], al_d, ALU.add).then_inc(col_step, 1)
                    dve.wait_ge(col_step, 5 * g + 4)
                    nc.vector.tensor_scalar(z_col[:, :], z_col[:, :], 0.0, (1 - SLOPE) / SLOPE, ALU.max, ALU.mult).then_inc(col_step, 1)
                    dve.wait_ge(col_step, 5 * g + 5)
                    nc.vector.tensor_tensor(z_col[:, :], z_col[:, :], row_cols[:, 0, :], ALU.add).then_inc(col_done, 1)
                    dve.wait_ge(col_done, g + 1)
                    nc.vector.tensor_scalar(row_cols[:, 1, :], z_col[:, :], SLOPE, None, ALU.mult).then_inc(cols_ready, 1)

                def exponent(l, c, t):
                    g = step_number(l, c)
                    if t == 0:
                        dve.wait_ge(rows_ready, g + 1)
                    dve.wait_ge(distance_ready, TILES * g + t + 1)
                    slot = ring[0:LANES, (TILES * c + t) % RING, :]
                    nc.vector.scalar_tensor_tensor(out=slot, in0=bent_row[:, parity(l, c), :], scalar=al_fifth[:, l.second, t:t + 1],
                                                   in1=slot, op0=ALU.subtract, op1=ALU.min).then_inc(exponent_ready, 1)

                def weigh(l, pair):
                    (c, t), (last_c, last_t) = divmod(pair[0], TILES), divmod(pair[-1], TILES)
                    together = c == last_c and not streamed
                    for these in [pair] if together else [[slot] for slot in pair]:
                        c, t = divmod(these[0], TILES)
                        n, first = len(these), these[0] % RING
                        dve.wait_ge(exp_ready, SLOTS * l.number + these[-1] + 1)
                        if streamed:
                            dve.wait_ge(weigh_tile_in, 16 * (SLOTS * l.number + these[0]) + 16)
                        code = weigh_tile[:, :].rearrange("p (o w) -> p o w", o=1) if streamed else counts[:, t:t + n, chunk_columns(c)]
                        slots = ring[0:LANES, first:first + n, :]
                        nc.vector.scalar_tensor_tensor(out=slots, in0=code, scalar=1.0, in1=slots,
                                                       op0=ALU.add, op1=ALU.mult).then_inc(weight_ready, n)

                def denominators(l, c):
                    g = step_number(l, c)
                    dve.wait_ge(tile_used, TILES * g + 2 * TILES)
                    dve.wait_ge(nodes_ready, g + CHUNKS)
                    for b, n in ((0, 3), (1, 2)):
                        last = nc.vector.tensor_scalar(
                            denom[:, 3 * b:3 * b + n],
                            psum[0:LANES, SUMS + 2 * parity(l, c) + b, 0:n * (FEAT + 1)].rearrange("p (i f) -> p i f", f=FEAT + 1)[:, :, FEAT],
                            2 * SOFTMAX_EPS, None, ALU.add)
                    last.then_inc(denom_step, 1)
                    dve.wait_ge(denom_step, g + 1)
                    nc.vector.reciprocal(denom[:, :], denom[:, :]).then_inc(denom_ready, 1)

                def add_x(c):
                    dve.wait_ge(sigmoid_ready, c + 1)
                    dve.wait_ge(x_again, 16 * c + 16)
                    nc.vector.tensor_tensor(result, result, x_chunk, ALU.add).then_inc(result_ready, 1)

                def layer(l):
                    last_layer = isinstance(l.number, int)
                    maxima_taken[0] = 0
                    slots = in_slots(last_layer)
                    for slot in range(EXPONENTS_AHEAD):
                        exponent(l, *divmod(slot, TILES))
                    for pair in PAIRS:
                        for slot in pair:
                            for m in slots[slot]:
                                take_max(l, m)
                            if slot == pair[-1]:
                                weigh(l, pair)
                            if slot + EXPONENTS_AHEAD < SLOTS:
                                exponent(l, *divmod(slot + EXPONENTS_AHEAD, TILES))
                        for c, t in (divmod(slot, TILES) for slot in pair):
                            if c and t == DENOMINATORS:
                                denominators(l, c - 1)
                            if c < CHUNKS - 1 and t == COLUMNS:
                                columns(l, c + 1)
                            if last_layer and c and t == ADD_X:
                                add_x(c - 1)
                    if last_layer:
                        denominators(l, CHUNKS - 1)
                        add_x(CHUNKS - 1)
                        return
                    for n, these in enumerate(AT_END):
                        for m in these:
                            take_max(l, m)
                        if n == 0:
                            denominators(l, CHUNKS - 1)
                        if n == 3:
                            columns(following(l), 0)

                normalise(0)
                normalise(1)
                for c in range(CHUNKS):
                    if c + 2 < CHUNKS:
                        normalise(c + 2)
                    for m in BEFORE_LAYERS:
                        if m[2] // PER == c:
                            take_max(FIRST, m, before_layers=True)
                columns(FIRST, 0)
                with dve.Fori(0, LAYERS // 2) as pair:
                    for second in range(2):
                        layer(Layer(2 * pair + second, second, pair))
                layer(LAST)

        @block.tensor
        def _(pe):
            with taken(pe, whole, whole_ready, when):
                def turn_nodes(f, rows_read=None, second=0):
                    pe.wait_ge(nodes_ready, f + 1)
                    if rows_read is not None:
                        pe.wait_ge(rows_ready, rows_read)
                    for i in range(PER):
                        last = nc.tensor.transpose(piece(FINISH + 2 * second, i, 128), nodes[second][:, i, :], ident[0:LANES, 0:LANES])
                    last.then_inc(nodes_turned, 1)

                def dense(w, second=0):
                    bank, x_t = FINISH + 2 * second, feats[second]
                    nc.tensor.matmul(psum[:, bank, 0:4 * LANES], w, x_t[:, 0:4 * LANES], start=True, stop=True)
                    nc.tensor.matmul(psum[:, bank + 1, 0:LANES], w, x_t[:, 4 * LANES:WIDE], start=True, stop=True).then_inc(dense_ready, 1)

                def make_hidden(f, k, first, frees_ring=False, second=0):
                    if first:
                        pe.wait_ge(weights_in, 32 * k + 32)
                    for i in range(PER):
                        at = (FEAT + 2) * (i % 3)
                        last = nc.tensor.matmul(psum[0:LANES, FINISH + 2 * second + i // 3, at:at + FEAT + 2],
                                                feats[second][:, LANES * i:LANES * (i + 1)],
                                                weights[:, :], start=True, stop=True)
                        if i == 0 and frees_ring:
                            last.then_inc(tile_used, TILES // CHUNKS)
                        if i < PER - 1:
                            yield
                    last.then_inc(hidden_mm, 1)
                    yield

                pe.wait_ge(consts_in, 64)
                for c, stage in ENCODER:
                    if stage == 0:
                        if c > 1:
                            pe.wait_ge(hidden_ready, c - 1)
                        turn_nodes(c, second=c % 2)
                    elif stage == 1:
                        pe.wait_ge(feats_ready, c + 1)
                        dense(enc_w[:, 0, :], c % 2)
                    elif stage < 4:
                        pe.wait_ge(dense_copied, dense_number(c, stage - 1) + 1)
                        dense(enc_w[:, stage - 1, :], c % 2)
                    else:
                        pe.wait_ge(dense_copied, dense_number(c, 3) + 1)
                        run(make_hidden(c, 0, c == 0, frees_ring=True, second=c % 2))

                def turn_largest(l, c):
                    g = step_number(l, c)
                    pe.wait_ge(*maxed_at(l, (0, c, TILES - 1)))
                    if not (isinstance(g, int) and g == 0):
                        pe.wait_ge(rows_ready, g)
                    if isinstance(l.number, int) and l.number == LAYERS - 1:
                        if c > 1:
                            pe.wait_ge(sigmoid_ready, c - 1)
                        pe.wait_ge(hidden_ready, CHUNKS * LAYERS)
                    else:
                        pe.wait_ge(hidden_ready, CHUNKS * (l.number + 1) + max(c - 1, 0))
                    for i in range(PER):
                        last = nc.tensor.transpose(piece(START, i), largest[:, parity(l, c), LANES * i:LANES * (i + 1)], ident[0:LANES, 0:LANES])
                    last.then_inc(largest_turned, 1)

                def spread_rows(l, c):
                    g = step_number(l, c)
                    pe.wait_ge(cols_ready, g + 1)
                    for q in range(2 * PER):
                        last = nc.tensor.transpose(piece(START, q), row_cols[:, q // PER, q % PER:q % PER + 1].broadcast_to([LANES, LANES]),
                                                   ident[0:LANES, 0:LANES])
                        if q % PER_BANK == PER_BANK - 1 or q == 2 * PER - 1:
                            last.then_inc(rows_spread, 1)
                            yield

                def add_tile(l, c, t):
                    g = step_number(l, c)
                    pe.wait_ge(weight_ready, TILES * g + t + 1)
                    if t == 0:
                        pe.wait_ge(nodes_ready, g + CHUNKS - 1)
                    for i in range(PER):
                        last = nc.tensor.matmul(sums(parity(l, c), i), ring[0:LANES, (TILES * c + t) % RING, LANES * i:LANES * (i + 1)],
                                                hidden[0:LANES, l.second, t, :], start=t == 0 and i % 3 == 0, stop=t == TILES - 1,
                                                skip_group_check=True)
                    last.then_inc(tile_used, 1)

                def rows_used(l, c):
                    return step_number(l, min(c + 1, CHUNKS - 1)) + 1

                def finish_next(l, c):
                    f = step_number(following(l), c)
                    turn_nodes(f, rows_used(l, c))
                    yield
                    pe.wait_ge(feats_ready, f + 1)
                    yield from make_hidden(f, l.number + 1, c == 0)

                def finish_decoder(c):
                    f = LAYERS * CHUNKS + c
                    turn_nodes(f, rows_used(LAST, c))
                    yield
                    pe.wait_ge(dec_in, 32)
                    pe.wait_ge(feats_ready, f + 1)
                    dense(dec_w[:, 0, :])
                    yield
                    pe.wait_ge(dense_copied, 3 * CHUNKS + 2 * c + 1)
                    dense(dec_w[:, 1, :])
                    yield
                    pe.wait_ge(dense_copied, 3 * CHUNKS + 2 * c + 2)
                    pe.wait_ge(ones_set, 3)
                    for i in range(PER):
                        at = psum[0:LANES, FINISH + i // 4, FEAT * (i % 4):FEAT * (i % 4 + 1)]
                        nc.tensor.matmul(at, feat_major[:, LANES * i:LANES * (i + 1)], dec_w[:, 2, :], start=i % 4 == 0, stop=False,
                                         skip_group_check=True)
                        last = nc.tensor.matmul(at, one_row, dec_row, start=False, stop=True, skip_group_check=True)
                    last.then_inc(hidden_mm, 1)
                    yield

                def layer(l):
                    last_layer = isinstance(l.number, int)
                    finish = lambda c: finish_decoder(c) if last_layer else finish_next(l, c)
                    for slot in range(SLOTS):
                        c, t = divmod(slot, TILES)
                        if c and t == 0:
                            parts = finish(c - 1)
                        if c:
                            for _ in range((DECODER_PE if last_layer else NEXT_PE).count(t)):
                                next(parts)
                        if c < CHUNKS - 1 and t == TURN_MAX:
                            turn_largest(l, c + 1)
                            spreading = spread_rows(l, c + 1)
                        if c < CHUNKS - 1:
                            for _ in range(SPREAD.count(t)):
                                next(spreading)
                        add_tile(l, c, t)
                    run(finish(CHUNKS - 1))
                    if not last_layer:
                        turn_largest(following(l), 0)
                        run(spread_rows(following(l), 0))

                pe.wait_ge(ones_set, 2)
                turn_largest(FIRST, 0)
                run(spread_rows(FIRST, 0))
                with pe.Fori(0, LAYERS // 2) as pair:
                    for second in range(2):
                        layer(Layer(2 * pair + second, second, pair))
                layer(LAST)

        @block.scalar
        def _(act):
            with taken(act, whole, whole_ready, when):
                def copy_features(func, bias, copied, second):
                    bank = FINISH + 2 * second
                    nc.scalar.activation(feats[second][:, 0:4 * LANES], psum[:, bank, 0:4 * LANES], func, bias=bias)
                    yield
                    nc.scalar.activation(feats[second][:, 4 * LANES:WIDE], psum[:, bank + 1, 0:LANES], func, bias=bias).then_inc(copied, 1)
                    yield

                def copy_feats(f, bias, second=0):
                    act.wait_ge(nodes_turned, f + 1)
                    yield from copy_features(ACT.Relu, bias, feats_ready, second)

                def copy_dense(number, func, bias, second=0):
                    act.wait_ge(dense_ready, number + 1)
                    yield from copy_features(func, bias, dense_copied, second)

                def copy_hidden(k, c, second=0):
                    f = step_number(k, c)
                    al_k, tiny_k, minus_k, fifth_k = (a[:, k.second] for a in (al, al_tiny, al_minus, al_fifth))
                    hidden_k = hidden[0:LANES, k.second]
                    act.wait_ge(hidden_mm, f + 1)
                    for i, n in ((0, 3), (1, 2)):
                        tiles = slice(PER * c + 3 * i, PER * c + 3 * i + n)
                        nc.scalar.activation(al_k[:, tiles, :], fresh(second, i, FEAT, FEAT + 2), ACT.Copy).then_inc(al_ready, 1)
                    own = slice(PER * c, PER * (c + 1))
                    act.wait_ge(al_ready, 2 * f + 2)
                    nc.scalar.mul(tiny_k[:, own], al_k[:, own, 0], TINY)
                    nc.scalar.mul(minus_k[:, own], al_k[:, own, 0], -1.0)
                    nc.scalar.mul(fifth_k[:, own], al_k[:, own, 0], SLOPE).then_inc(al_scaled, 1)
                    yield
                    nc.scalar.activation(hidden_k[:, PER * c:PER * c + 3, 0:FEAT], fresh(second, 0, 0, FEAT), ACT.Copy)
                    yield
                    nc.scalar.activation(hidden_k[:, PER * c + 3:PER * (c + 1), 0:FEAT], fresh(second, 1, 0, FEAT), ACT.Copy).then_inc(hidden_ready, 1)
                    yield

                act.wait_ge(consts_in, 64)
                act.wait_ge(variance_ready, 1)
                nc.scalar.activation(spread[:, 1, :], spread[:, 0, :], ACT.Sqrt).then_inc(root_ready, 1)
                for c, stage in ENCODER:
                    if stage == 0:
                        run(copy_feats(c, 0.0, c % 2))
                    elif stage < 4:
                        run(copy_dense(dense_number(c, stage), ACT.Relu if stage < 3 else ACT.Identity,
                                       enc_bias[:, stage - 1:stage], c % 2))
                    else:
                        run(copy_hidden(FIRST, c, c % 2))

                def copy_rows(l, c):
                    g = step_number(l, c)
                    if not (isinstance(g, int) and g == 0):
                        act.wait_ge(distance_ready, TILES * g)
                    bent = bent_row[:, parity(l, c), :]
                    act.wait_ge(rows_spread, 3 * g + 1)
                    nc.scalar.activation(top_row[:, 0:4 * LANES], psum[0:LANES, START, 0:4 * LANES], ACT.Copy)
                    act.wait_ge(rows_spread, 3 * g + 2)
                    nc.scalar.activation(top_row[:, 4 * LANES:WIDE], psum[0:LANES, START + 1, 0:LANES], ACT.Copy)
                    nc.scalar.activation(bent[:, 0:3 * LANES], psum[0:LANES, START + 1, LANES:4 * LANES], ACT.Copy)
                    act.wait_ge(rows_spread, 3 * g + 3)
                    last = nc.scalar.activation(bent[:, 3 * LANES:WIDE], psum[0:LANES, START + 2, 0:2 * LANES], ACT.Copy)
                    last.then_inc(rows_ready, 1)

                def distance(l, c, t):
                    slot = TILES * c + t
                    act.wait_ge(tile_used, TILES + SLOTS * l.number + max(slot - RING + 1, 0))
                    if t == 0:
                        act.wait_ge(rows_ready, step_number(l, c) + 1)
                    nc.scalar.activation(ring[0:LANES, (TILES * c + t) % RING, :], top_row[:, :], ACT.Identity,
                                         bias=al_minus[:, l.second, t:t + 1]).then_inc(distance_ready, 1)

                def clamp(l, pair):
                    act.wait_ge(exponent_ready, SLOTS * l.number + pair[-1] + 1)
                    slots = ring[0:LANES, pair[0] % RING:pair[0] % RING + len(pair), :]
                    nc.scalar.activation(slots, slots, ACT.Relu).then_inc(clamped, len(pair))

                def exp(l, pair):
                    act.wait_ge(clamped, SLOTS * l.number + pair[-1] + 1)
                    slots = ring[0:LANES, pair[0] % RING:pair[0] % RING + len(pair), :]
                    nc.scalar.activation(slots, slots, ACT.Exp, scale=-1.0).then_inc(exp_ready, len(pair))

                def divide(l, c):
                    g = step_number(l, c)
                    act.wait_ge(denom_ready, g + 1)
                    act.wait_ge(nodes_turned, g + CHUNKS)
                    for i in range(PER):
                        last = nc.scalar.activation(node_major[:, i, :], sums(parity(l, c), i, 0, FEAT), ACT.Copy, scale=denom[:, i:i + 1])
                        if i < PER - 1:
                            yield
                    last.then_inc(nodes_ready, 1)
                    yield

                def finish_next(l, c):
                    yield from divide(l, c)
                    yield from copy_feats(step_number(following(l), c), conv_bias[:, bass.ds(l.number, 1)])
                    yield from copy_hidden(following(l), c)

                def finish_decoder(c):
                    yield from divide(LAST, c)
                    yield from copy_feats(LAYERS * CHUNKS + c, conv_bias[:, LAYERS - 1:LAYERS])
                    for k in range(2):
                        yield from copy_dense(3 * CHUNKS + 2 * c + k, ACT.Relu, dec_bias[:, k:k + 1])
                    act.wait_ge(hidden_mm, LAYERS * CHUNKS + c + 1)
                    act.wait_ge(dec_in, 32)
                    if c:
                        act.wait_ge(stored, 16 * c)
                    nc.scalar.activation(result[:, 0:4 * FEAT], psum[0:LANES, FINISH, 0:4 * FEAT], ACT.Sigmoid)
                    yield
                    nc.scalar.activation(result[:, 4 * FEAT:5 * FEAT], psum[0:LANES, FINISH + 1, 0:FEAT], ACT.Sigmoid).then_inc(sigmoid_ready, 1)
                    yield

                def layer(l):
                    last_layer = isinstance(l.number, int)
                    finish = lambda c: finish_decoder(c) if last_layer else finish_next(l, c)
                    for slot in range(LEAD):
                        distance(l, *divmod(slot, TILES))
                    clamp(l, PAIRS[0])
                    for n, pair in enumerate(PAIRS):
                        exp(l, pair)
                        if n + 1 < len(PAIRS):
                            clamp(l, PAIRS[n + 1])
                        for slot in pair:
                            c, t = divmod(slot + LEAD, TILES)
                            if t == 0 and c < CHUNKS:
                                copy_rows(l, c)
                            if c < CHUNKS:
                                distance(l, c, t)
                        for c, t in (divmod(slot, TILES) for slot in pair):
                            if c and t == 0:
                                parts = finish(c - 1)
                            if c:
                                for _ in range((DECODER_ACT if last_layer else NEXT_ACT).count(t)):
                                    next(parts)
                    run(finish(CHUNKS - 1))
                    if not last_layer:
                        copy_rows(following(l), 0)

                copy_rows(FIRST, 0)
                with act.Fori(0, LAYERS // 2) as pair:
                    for second in range(2):
                        layer(Layer(2 * pair + second, second, pair))
                layer(LAST)


Layer = namedtuple("Layer", "number second pair")
FIRST, LAST = Layer(0, 0, 0), Layer(LAYERS - 1, 0, LAYERS // 2)


def following(l):
    return Layer(l.number + 1, 1 - l.second, l.pair + l.second)


def step_number(l, c):
    return CHUNKS * l.number + c


def parity(l, c):
    return (CHUNKS * l.second + c) % 2


def alike_before(l, c):
    return CHUNKS * l.pair + (CHUNKS * l.second + c) // 2


def tile_range(c):
    return slice(PER * c, PER * (c + 1))


def chunk_columns(c):
    return slice(WIDE * c, WIDE * (c + 1))


_INS = ["x", "src", "dst", "L0_gnn_enc_W", "L0_gnn_enc_b", "L0_gnn_conv_W", "L0_gnn_conv_att_src",
        "L0_gnn_conv_att_dst", "L0_gnn_conv_b", "L0_gnn_dec_W", "L0_gnn_dec_b"]


def kernel(**inputs):
    import numpy as _np
    import concourse.bacc as _bacc
    from concourse import mybir as _mybir
    from concourse.bass_utils import run_bass_kernel_spmd as _run

    nc = _bacc.Bacc("TRN2", target_bir_lowering=False, num_devices=1)
    arrays, args = {}, []
    for name in _INS:
        a = _np.ascontiguousarray(inputs[name])
        arrays[f"in_{name}"] = a
        args.append(nc.dram_tensor(f"in_{name}", a.shape, _mybir.dt.from_np(a.dtype), kind="ExternalInput").ap())
    args.append(nc.dram_tensor("out_0", (NODES, FEAT), F32, kind="ExternalOutput").ap())
    nc.disable_value_cache = True
    gat_program(nc, *args)
    r = _run(nc, [arrays], core_ids=[0])
    return r.results[0]["out_0"]
```
